# Optimizing a Trainium2 kernel written in Bass

```python
import numpy as np
import jax
import jax.numpy as jnp

def _softmax(x, axis=-1):
    return jax.nn.softmax(x, axis=axis)

def _gelu(x):
    return jax.nn.gelu(x, approximate=True)

def _silu(x):
    return jax.nn.silu(x)

def _sigmoid(x):
    return jax.nn.sigmoid(x)

def _layernorm(x, axis=-1, eps=1e-05):
    m = jnp.mean(x, axis=axis, keepdims=True)
    v = jnp.var(x, axis=axis, keepdims=True)
    return (x - m) / jnp.sqrt(v + eps)

def _scatter_add(tgt, idx, src, axis=0):
    return tgt.at[idx].add(src)

def _segment_sum(src, seg, n):
    return jax.ops.segment_sum(src, seg, n)
kernel_name = 'mk_vit_tower_d1_tok_img768_r4_b1ee18'

def setup_inputs(seed: int=0):
    np.random.seed(seed)
    _w = jnp.asarray

    def _rec_inputs():
        import jax
        import jax.numpy as jnp
        _rk = jax.random.key(seed)
        x = -0.00016672 + 0.999947 * jax.random.normal(jax.random.fold_in(_rk, 1), (64, 96, 96, 3), jnp.float32)
        return x
    x = _rec_inputs()

    def _L0_tok_setup():
        import jax, jax.numpy as jnp
        import numpy as np
        PATCH = 16
        IMG = 96
        NP_ = (IMG // PATCH) ** 2
        DIM = 192
        BATCH = 64
        key = jax.random.key(seed)
        k1, k2, k3, k4 = jax.random.split(key, 4)
        x = jax.random.normal(k1, (BATCH, IMG, IMG, 3), dtype=jnp.float32)
        in_dim = PATCH * PATCH * 3
        W = jax.random.normal(k2, (in_dim, DIM), dtype=jnp.float32) * (1.0 / np.sqrt(in_dim))
        b = jnp.zeros((DIM,), dtype=jnp.float32)
        cls_token = jax.random.normal(k3, (1, 1, DIM), dtype=jnp.float32) * 0.02
        pos_table = jax.random.normal(k4, (NP_ + 1, DIM), dtype=jnp.float32) * 0.02
        return {'x': x, 'W': W, 'b': b, 'cls_token': cls_token, 'pos_table': pos_table}
    _L0_tok_all = _L0_tok_setup()
    _L0_tok_in = {k: v for k, v in _L0_tok_all.items() if k in ('W', 'b', 'cls_token', 'pos_table')}
    del _L0_tok_all

    def _L0_attn_setup():
        import jax, jax.numpy as jnp
        import numpy as np
        H = 12
        E = 192
        LORA_SCALE = 32.0 / 4.0
        NEG = -1000000000.0
        key = jax.random.key(seed)
        ks = jax.random.split(key, 8)
        B, L = (2, 512)
        return {'x': jax.random.normal(ks[0], (B, L, E), jnp.float32), 'w_in': jax.random.normal(ks[1], (E, 3 * E), jnp.float32) * 0.02, 'b_in': jnp.zeros((3 * E,), jnp.float32), 'A_in': jax.random.normal(ks[2], (4, 3 * E), jnp.float32) * 0.02, 'B_in': jax.random.normal(ks[3], (E, 4), jnp.float32) * 0.02, 'w_out': jax.random.normal(ks[4], (E, E), jnp.float32) * 0.02, 'b_out': jnp.zeros((E,), jnp.float32), 'A_out': jax.random.normal(ks[5], (4, E), jnp.float32) * 0.02, 'B_out': jax.random.normal(ks[6], (E, 4), jnp.float32) * 0.02}
    _L0_attn_all = _L0_attn_setup()
    _L0_attn_in = {k: v for k, v in _L0_attn_all.items() if k in ('w_in', 'b_in', 'A_in', 'B_in', 'w_out', 'b_out', 'A_out', 'B_out')}
    del _L0_attn_all

    def _L0_ffn_setup():
        import jax, jax.numpy as jnp
        import numpy as np
        B, T, H, F, E = (128, 32, 192, 768, 3)
        key = jax.random.key(seed)
        ks = jax.random.split(key, 4)
        s = 0.02
        return {'x': jax.random.normal(ks[0], (B, T, H), jnp.float32), 'Wg': jax.random.normal(ks[1], (E, H), jnp.float32) * s, 'W1': jax.random.normal(ks[2], (E, H, F), jnp.float32) * s, 'b1': jnp.zeros((E, F), jnp.float32), 'W2': jax.random.normal(ks[3], (E, F, H), jnp.float32) * s, 'b2': jnp.zeros((E, H), jnp.float32)}
    _L0_ffn_all = _L0_ffn_setup()
    _L0_ffn_in = {k: v for k, v in _L0_ffn_all.items() if k in ('Wg', 'W1', 'b1', 'W2', 'b2')}
    del _L0_ffn_all
    return {'x': x, 'L0_tok_W': _L0_tok_in['W'], 'L0_tok_b': _L0_tok_in['b'], 'L0_tok_cls_token': _L0_tok_in['cls_token'], 'L0_tok_pos_table': _L0_tok_in['pos_table'], 'L0_attn_w_in': _L0_attn_in['w_in'], 'L0_attn_b_in': _L0_attn_in['b_in'], 'L0_attn_A_in': _L0_attn_in['A_in'], 'L0_attn_B_in': _L0_attn_in['B_in'], 'L0_attn_w_out': _L0_attn_in['w_out'], 'L0_attn_b_out': _L0_attn_in['b_out'], 'L0_attn_A_out': _L0_attn_in['A_out'], 'L0_attn_B_out': _L0_attn_in['B_out'], 'L0_ffn_Wg': _L0_ffn_in['Wg'], 'L0_ffn_W1': _L0_ffn_in['W1'], 'L0_ffn_b1': _L0_ffn_in['b1'], 'L0_ffn_W2': _L0_ffn_in['W2'], 'L0_ffn_b2': _L0_ffn_in['b2']}

def reference(x, L0_tok_W, L0_tok_b, L0_tok_cls_token, L0_tok_pos_table, L0_attn_w_in, L0_attn_b_in, L0_attn_A_in, L0_attn_B_in, L0_attn_w_out, L0_attn_b_out, L0_attn_A_out, L0_attn_B_out, L0_ffn_Wg, L0_ffn_W1, L0_ffn_b1, L0_ffn_W2, L0_ffn_b2):
    import jax
    import jax.numpy as jnp

    def _L0_tok_ref(x, W, b, cls_token, pos_table):
        import jax, jax.numpy as jnp
        import numpy as np
        PATCH = 16
        IMG = 96
        NP_ = (IMG // PATCH) ** 2
        DIM = 192
        BATCH = 64
        B, H, Wd, C = x.shape
        gh, gw = (H // PATCH, Wd // PATCH)
        patches = x.reshape(B, gh, PATCH, gw, PATCH, C)
        patches = patches.transpose(0, 1, 3, 2, 4, 5)
        patches = patches.reshape(B, gh * gw, PATCH * PATCH * C)
        proj = jnp.einsum('bnd,de->bne', patches, W) + b
        cls = jnp.broadcast_to(cls_token, (B, 1, proj.shape[-1]))
        tokens = jnp.concatenate([cls, proj], axis=1)
        return tokens + pos_table[None, :, :]

    def _L0_attn_ref(x, w_in, b_in, A_in, B_in, w_out, b_out, A_out, B_out):
        import jax, jax.numpy as jnp
        import numpy as np
        H = 12
        E = 192
        LORA_SCALE = 32.0 / 4.0
        NEG = -1000000000.0
        Bb, L, _ = x.shape
        D = E // H
        w1 = w_in + LORA_SCALE * (B_in @ A_in)
        c = jnp.einsum('ble,eo->blo', x, w1) + b_in
        q, k, v = jnp.split(c, 3, axis=2)

        def heads(t):
            return t.reshape(Bb, L, H, D).transpose(0, 2, 1, 3)
        q, k, v = (heads(q), heads(k), heads(v))
        w = jnp.einsum('bhqd,bhkd->bhqk', q, k)
        band = jnp.tril(jnp.ones((L, L), jnp.float32))
        w = w * band + NEG * (1.0 - band)
        w = jax.nn.softmax(w, axis=-1)
        a = jnp.einsum('bhqk,bhkd->bhqd', w, v)
        a = a.transpose(0, 2, 1, 3).reshape(Bb, L, E)
        w2 = w_out + LORA_SCALE * (B_out @ A_out)
        return jnp.einsum('ble,eo->blo', a, w2) + b_out

    def _L0_ffn_ref(x, Wg, W1, b1, W2, b2):
        import jax, jax.numpy as jnp
        import numpy as np
        B, T, H, F, E = (128, 32, 192, 768, 3)
        scores = jax.nn.softmax(jnp.mean(x, axis=1) @ Wg.T, axis=-1)
        _, idx = jax.lax.top_k(scores, 1)
        sel = idx[:, 0]
        h = jax.nn.gelu(jnp.einsum('bth,ehf->betf', x, W1) + b1[None, :, None, :], approximate=False)
        y = jnp.einsum('betf,efh->beth', h, W2) + b2[None, :, None, :]
        w = scores * jax.nn.one_hot(sel, E, dtype=scores.dtype)
        out = jnp.einsum('beth,be->bth', y, w)
        return out
    h = _L0_tok_ref(x, L0_tok_W, L0_tok_b, L0_tok_cls_token, L0_tok_pos_table)
    h = h + _L0_attn_ref(_layernorm(h, axis=-1), L0_attn_w_in, L0_attn_b_in, L0_attn_A_in, L0_attn_B_in, L0_attn_w_out, L0_attn_b_out, L0_attn_A_out, L0_attn_B_out)
    h = h + _L0_ffn_ref(_layernorm(h, axis=-1), L0_ffn_Wg, L0_ffn_W1, L0_ffn_b1, L0_ffn_W2, L0_ffn_b2)
    return h

_drawn_inputs = setup_inputs


def setup_inputs(seed=0):
    import zlib

    import numpy as np

    out = dict(_drawn_inputs(seed))
    spreads = {'L0_tok_b': (0.0, 0.1),
     'L0_attn_b_in': (0.0, 0.1),
     'L0_attn_b_out': (0.0, 0.1),
     'L0_ffn_b1': (0.0, 0.746),
     'L0_ffn_b2': (0.0, 0.639)}
    factors = {'L0_tok_cls_token': 3.361,
     'L0_attn_A_in': 5.594,
     'L0_attn_B_in': 5.375,
     'L0_attn_A_out': 2.998,
     'L0_attn_B_out': 2.845,
     'L0_ffn_W1': 4.353}
    for name, (base, spread) in spreads.items():
        noise = np.random.default_rng([zlib.crc32(name.encode()), seed]).standard_normal(out[name].shape)
        drawn = base * np.exp(spread * noise) if base else spread * noise
        out[name] = jnp.asarray(drawn.astype(out[name].dtype))
    for name, factor in factors.items():
        out[name] = (out[name] * factor).astype(out[name].dtype)
    return out
```

```python
from contextlib import ExitStack

import numpy as np

import concourse.bass as bass
from concourse import mybir

F32 = mybir.dt.float32
F16 = mybir.dt.float16
BF16 = mybir.dt.bfloat16
I32 = mybir.dt.int32
ALU = mybir.AluOpType
ACT = mybir.ActivationFunctionType
AX = mybir.AxisListType.X

IMAGES = 64
PATCH = 16
GRID = 6
TOK = GRID * GRID + 1
PIX = PATCH * PATCH * 3
PK = PIX // 128
DIM = 192
HD = DIM // 2
HEADS = 12
HDIM = DIM // HEADS
HP = HEADS // 2
FFN = 768
FM = FFN // 128
EXPERTS = 3
LORA = 8.0
EPS = 1e-5
SPLIT = 64.0

GI = 8
NG = IMAGES // GI
GT = GI * TOK
TI = 3
TT = TI * TOK
TILES = -(-GI // TI)
GW = TILES * TT
PAIRS = GI // 2
SLOT = 64

BI = 9
BW = BI * TOK
BLOCKS = (IMAGES + EXPERTS * (BI - 1)) // BI
ROUND = 8


def vit_layer(nc, x, tok_w, row_add, pos_rows, w_in, lora_in, w_out, lora_out, b_qkv, b_out, head_sel, causal,
              ident32, wg, w1, b1, w2, b2, order, tile_sel, slot_sel, steps, out):
    with ExitStack() as ctx:
        def sb(name, shape, dt=F32):
            return ctx.enter_context(nc.sbuf_tensor(name, shape, dt))

        def sem(name):
            return ctx.enter_context(nc.semaphore(name))

        at = bass.ds

        score_ps = [ctx.enter_context(nc.psum_tensor(f"score_ps{i}", [128, 512], F32)) for i in range(2)]
        turn_ps = [ctx.enter_context(nc.psum_tensor(f"turn_ps{i}", [128, 512], F32)) for i in range(2)]
        att_ps = [ctx.enter_context(nc.psum_tensor(f"att_ps{i}", [128, 512], F32)) for i in range(2)]
        work_ps = [ctx.enter_context(nc.psum_tensor(f"work_ps{i}", [128, 512], F32)) for i in range(2)]

        gelu_ps = [*score_ps, *turn_ps, *work_ps]
        y_ps = att_ps

        early = sb("early", [128, PK * GW + PK * DIM + 2 * 3 * DIM])
        x_sb = early[:, 0:PK * GW].rearrange("p (k t) -> p k t", k=PK)
        tok_w_sb = early[:, PK * GW:PK * (GW + DIM)].rearrange("p (k d) -> p k d", k=PK)
        row_add_sb = sb("row_add_sb", [TT, DIM])
        pos_sb = sb("pos_sb", [TT, DIM])
        w_in_sb = early[0:HD, PK * (GW + DIM):].rearrange("p (k d) -> p k d", k=2)
        lora_in_sb = sb("lora_in_sb", [4, DIM + 3 * DIM])
        w_out_sb = sb("w_out_sb", [HD, 2, DIM])
        lora_out_sb = sb("lora_out_sb", [4, 2 * DIM])
        qkv_hl = sb("qkv_hl", [HD, 2, 2, 3 * DIM], F16)
        b_qkv_sb = sb("b_qkv_sb", [HD, 6])
        b_out_sb = sb("b_out_sb", [TT, DIM])
        head_sel_sb = sb("head_sel_sb", [HD, HP])
        causal_sb = sb("causal_sb", [128, HEADS * TOK], BF16)
        ident16_sb = sb("ident16_sb", [128, 128], BF16)
        ident32_sb = sb("ident32_sb", [128, 128])
        wg_sb = sb("wg_sb", [HD, 2, EXPERTS])
        staged = sb("staged", [128, EXPERTS * (2 * FFN + FM * DIM)])
        w1_sb = staged[0:HD, 0:EXPERTS * 2 * FFN]
        w2_sb = staged[:, EXPERTS * 2 * FFN:]
        w1_hl = sb("w1_hl", [HD, 2, EXPERTS * 2 * FFN], F16)
        w2_hl = sb("w2_hl", [128, 2, EXPERTS * FM * DIM], F16)
        b1_sb = sb("b1_sb", [128, EXPERTS * FM])
        b2_sb = sb("b2_sb", [HD, EXPERTS * 2])
        order_sb = sb("order_sb", [IMAGES, 2 * IMAGES])
        tile_sel_sb = sb("tile_sel_sb", [IMAGES, NG * TILES])
        slot_sel_sb = sb("slot_sel_sb", [IMAGES, TT])
        steps_sb = sb("steps_sb", [IMAGES, ROUND + BLOCKS])

        h = sb("h", [TT, NG * TILES, DIM])
        stats = [sb(f"stats{i}", [TT, TILES, 6]) for i in range(2)]
        mean_var = [sb(f"mean_var{i}", [TT, TILES, 2]) for i in range(2)]
        var_eps = [sb(f"var_eps{i}", [TT, TILES]) for i in range(2)]
        rstd = [sb(f"rstd{i}", [TT, TILES]) for i in range(2)]
        neg_half = sb("neg_half", [TT, TILES])
        eps_sb = sb("eps_sb", [TT, TILES])
        xn = [sb(f"xn{i}", [TT, TILES, DIM]) for i in range(2)]
        xn_t = sb("xn_t", [HD, 2, 2, GW], F16)
        q_t = sb("q_t", [HD, 2, GW])
        k_t = sb("k_t", [HD, 2, GT])
        k_x = sb("k_x", [HD, 2, GI, HP, TOK])
        v_bd = sb("v_bd", [128, GI, HP, 2, HDIM])
        row_max = [sb(f"row_max{i}", [128, HEADS]) for i in range(2)]
        shifted = [sb(f"shifted{i}", [128, HEADS, TOK]) for i in range(2)]
        prob = [sb(f"prob{i}", [128, HEADS, SLOT]) for i in range(2)]
        row_sum = [sb(f"row_sum{i}", [128, HEADS]) for i in range(2)]
        inv_sum = [sb(f"inv_sum{i}", [128, HEADS]) for i in range(2)]
        prob_t = sb("prob_t", [128, HP, 2, TOK])
        att_t = sb("att_t", [HD, 2, GW])

        xs = sb("xs", [HD, 4, IMAGES * TOK], F16)
        x_sum = sb("x_sum", [HD, 2, IMAGES])
        x_sorted = sb("x_sorted", [HD, 4, BLOCKS * BW], F16)
        logit = sb("logit", [IMAGES, EXPERTS])
        top = sb("top", [IMAGES, 1])
        logit_s = sb("logit_s", [IMAGES, EXPERTS])
        score_e = sb("score_e", [IMAGES, EXPERTS])
        score_s = sb("score_s", [IMAGES, 1])
        gate = sb("gate", [IMAGES, 1])
        is_top = sb("is_top", [IMAGES, EXPERTS])
        not_first = sb("not_first", [IMAGES, 1])
        chosen = sb("chosen", [IMAGES, EXPERTS])
        over = sb("over", [IMAGES, EXPERTS, ROUND])
        n_block = sb("n_block", [IMAGES, EXPERTS])
        start = sb("start", [IMAGES, EXPERTS])
        place_e = sb("place_e", [IMAGES, EXPERTS])
        place_c = sb("place_c", [IMAGES, EXPERTS])
        place = sb("place", [IMAGES, 1])
        gate_tile = sb("gate_tile", [IMAGES, NG * TILES])
        gate_tok = sb("gate_tok", [TT, NG * TILES])
        begun = sb("begun", [1, 2, BLOCKS])
        place_i = sb("place_i", [1, IMAGES], I32)
        expert_i = sb("expert_i", [1, BLOCKS], I32)
        hid = [sb(f"hid{i}", [128, BW]) for i in range(2)]
        hid_hl = early[:, 0:2 * FM * BW].bitcast(F16)\
            .rearrange("p (b k m t) -> p b k m t", b=2, k=2, m=FM)
        y_sorted = staged[0:HD, 0:2 * BLOCKS * BW].rearrange("p (c t) -> p c t", c=2)
        q_flat = q_t[:].rearrange("p c t -> p (c t)")
        y_tile = [q_flat[:, i * 2 * TT:(i + 1) * 2 * TT].rearrange("p (c t) -> p c t", c=2) for i in range(3)]
        out_sb = [xn[i][:, t, :] for i in range(2) for t in range(TILES)]
        OUTS = len(out_sb)

        x_loaded = sem("x_loaded")
        attn_loaded = sem("attn_loaded")
        expert_loaded = sem("expert_loaded")
        zeroed = sem("zeroed")
        pos_added = sem("pos_added")
        mask_ready = sem("mask_ready")
        lora_done = sem("lora_done")
        qkv_full = sem("qkv_full")
        qkv_high = sem("qkv_high")
        qkv_low = sem("qkv_low")
        out_full = sem("out_full")
        embedded = sem("embedded")
        h_ready = sem("h_ready")
        stats_done = [sem(f"stats_done{i}") for i in range(2)]
        aggr_done = [sem(f"aggr_done{i}") for i in range(2)]
        eps_added = [sem(f"eps_added{i}") for i in range(2)]
        rstd_done = [sem(f"rstd_done{i}") for i in range(2)]
        xn_ready = [sem(f"xn_ready{i}") for i in range(2)]
        xn_turned = [sem(f"xn_turned{i}") for i in range(2)]
        xt_high = [sem(f"xt_high{i}") for i in range(2)]
        xt_low = [sem(f"xt_low{i}") for i in range(2)]
        token_sum = sem("token_sum")
        bias_added = sem("bias_added")
        q_done = sem("q_done")
        q_copied = sem("q_copied")
        k_done = sem("k_done")
        k_copied = sem("k_copied")
        k_spread_dve = sem("k_spread_dve")
        k_spread_pool = sem("k_spread_pool")
        v_done = sem("v_done")
        v_act = sem("v_act")
        v_dve = sem("v_dve")
        scored = sem("scored")
        max_done = sem("max_done")
        shift_done = sem("shift_done")
        exp_done = sem("exp_done")
        sum_done = sem("sum_done")
        inv_done = sem("inv_done")
        prob_ready = sem("prob_ready")
        prob_turned = sem("prob_turned")
        prob_copied = sem("prob_copied")
        att_done = sem("att_done")
        att_copied = sem("att_copied")
        projected = sem("projected")
        h2_ready = sem("h2_ready")
        w_high = sem("w_high")
        w_low = sem("w_low")
        logits_done = sem("logits_done")
        routing = sem("routing")
        scores_exp = sem("scores_exp")
        ranked = sem("ranked")
        placed = sem("placed")
        gates_spread = sem("gates_spread")
        gates_ready = sem("gates_ready")
        places_ready = sem("places_ready")
        sorted_dve = sem("sorted_dve")
        sorted_act = sem("sorted_act")
        hid_done = sem("hid_done")
        gelu_done = sem("gelu_done")
        hid_high = sem("hid_high")
        hid_low = sem("hid_low")
        y_done = sem("y_done")
        y_copied = sem("y_copied")
        picked_act = sem("picked_act")
        picked_dve = sem("picked_dve")
        y_turned = sem("y_turned")
        out_ready = sem("out_ready")
        stored = [sem(f"stored{i}") for i in range(2 * TILES)]

        block = ctx.enter_context(nc.Block())
        ATTN_LOADS = 14
        POOL_HEADS = 4
        EXPERT_LOADS = 9
        SLICE1 = EXPERTS * 2 * FFN // NG
        SLICE2 = EXPERTS * FM * DIM // NG
        TAILS = [GI - TI * t if GI < TI * (t + 1) else TI for t in range(TILES)]

        def spread(eng, c, a, b):
            n = b - a
            return eng.tensor_tensor(k_x[:, c, :, a:b, :],
                                     k_t[:, c, :].rearrange("p (i k) -> p i k", k=TOK).unsqueeze(2)
                                     .broadcast_to([HD, GI, n, TOK]),
                                     head_sel_sb[:, a:b].unsqueeze(1).unsqueeze(3).broadcast_to([HD, GI, n, TOK]),
                                     ALU.mult)

        @block.sync
        def _(sp):
            sp.dma_start(tok_w_sb[:], tok_w).then_inc(attn_loaded, 16)
            sp.dma_start(x_sb[:, :, 0:GT], x[0]).then_inc(x_loaded, 16)
            for dst, src in ((row_add_sb, row_add), (pos_sb, pos_rows), (w_in_sb, w_in), (lora_in_sb, lora_in),
                             (w_out_sb, w_out), (lora_out_sb, lora_out), (b_qkv_sb, b_qkv), (b_out_sb, b_out),
                             (head_sel_sb, head_sel), (shifted[0].rearrange("p a k -> p (a k)"), causal),
                             (ident32_sb, ident32), (wg_sb, wg), (order_sb, order)):
                sp.dma_start(dst[:], src).then_inc(attn_loaded, 16)
            sp.wait_ge(embedded, 2)
            sp.dma_start(x_sb[:, :, 0:GT], x[1]).then_inc(x_loaded, 16)
            for dst, src in ((w1_sb, w1), (w2_sb, w2), (b1_sb, b1), (b2_sb, b2), (tile_sel_sb, tile_sel),
                             (slot_sel_sb, slot_sel), (steps_sb, steps)):
                sp.dma_start(dst[:], src).then_inc(expert_loaded, 16)
            with sp.Fori(2, NG) as g:
                sp.wait_ge(embedded, g * 2)
                sp.dma_start(x_sb[:, :, 0:GT], x[at(g, 1)].rearrange("a p k t -> (a p) k t")).then_inc(x_loaded, 16)
            for t in range(NG * TILES):
                n = TAILS[t % TILES] * TOK
                row = (t // TILES * GI + t % TILES * TI) * TOK
                sp.wait_ge(out_ready, t + 1)
                sp.dma_start(out[row:row + n, :], out_sb[t % OUTS][0:n, :]).then_inc(stored[t % OUTS], 16)
            for i in range(OUTS):
                sp.wait_ge(stored[i], 16 * (NG * TILES // OUTS))

        @block.gpsimd
        def _(pool):
            pool.memset(x_sb[:, :, GT:GW], 0.0).then_inc(zeroed, 1)
            pool.memset(neg_half[:], -0.5).then_inc(zeroed, 1)
            pool.memset(eps_sb[:], EPS).then_inc(zeroed, 1)
            pool.memset(v_bd[:], 0.0).then_inc(zeroed, 1)
            for i in range(2):
                pool.memset(prob[i][:], 0.0).then_inc(zeroed, 1)
            pool.memset(att_t[:, :, GT:GW], 0.0).then_inc(zeroed, 1)
            pool.wait_ge(attn_loaded, 16 * ATTN_LOADS)
            pool.tensor_tensor(pos_sb[:], pos_sb[:], row_add_sb[:], ALU.add).then_inc(pos_added, 1)
            pool.tensor_copy(causal_sb[:], shifted[0][:].rearrange("p a k -> p (a k)")).then_inc(mask_ready, 1)
            pool.tensor_copy(ident16_sb[:], ident32_sb[:]).then_inc(mask_ready, 1)
            pool.memset(x_sorted[:], 0.0).then_inc(zeroed, 1)

            def inverse_std(n, w):
                pool.wait_ge(aggr_done[w], TILES * n + TILES)
                pool.tensor_tensor(var_eps[w][:], mean_var[w][:, :, 1], eps_sb[:], ALU.add).then_inc(eps_added[w], 1)
                pool.wait_ge(eps_added[w], n + 1)
                pool.tensor_tensor(rstd[w][:], var_eps[w][:], neg_half[:], ALU.pow).then_inc(rstd_done[w], 1)

            def normalise(g, p):
                pool.wait_ge(inv_done, PAIRS * g + p + 1)
                pr = prob[p % 2][:, :, 0:TOK]
                pool.tensor_tensor(pr, pr, inv_sum[p % 2][:].unsqueeze(2).broadcast_to([128, HEADS, TOK]),
                                   ALU.mult).then_inc(prob_ready, 1)

            def add_out_bias(n):
                pool.wait_ge(xn_ready[0], TILES * n + TILES)
                ht = h[:, at(n * TILES, TILES), :]
                pool.tensor_tensor(ht, ht, b_out_sb[:].unsqueeze(1).broadcast_to([TT, TILES, DIM]), ALU.add)\
                    .then_inc(bias_added, 1)

            def spread_keys(n):
                for c in range(2):
                    pool.wait_ge(k_copied, n * 2 + c + 1)
                    spread(pool, c, POOL_HEADS, HP).then_inc(k_spread_pool, 1)

            def group(g, first, last):
                if not first:
                    inverse_std(g - 1, 1)
                normalise(g, 0)
                if not last:
                    inverse_std(g + 1, 0)
                normalise(g, 1)
                if not last:
                    add_out_bias(g + 1)
                normalise(g, 2)
                normalise(g, 3)
                if not last:
                    spread_keys(g + 1)

            inverse_std(0, 0)
            add_out_bias(0)
            spread_keys(0)
            pool.wait_ge(zeroed, 8)
            group(0, True, False)
            with pool.Fori(1, NG - 1) as g:
                group(g, False, False)
            group(NG - 1, False, True)
            inverse_std(NG - 1, 1)

        @block.scalar
        def _(act):
            def copy_halves(n):
                for c in range(2):
                    act.wait_ge(xn_turned[0], 2 * n + c + 1)
                    act.activation(xn_t[:, 0, c, :], work_ps[c][0:HD, 0:GW], ACT.Copy).then_inc(xt_high[0], 1)

            def copy_qk(n):
                for c in range(2):
                    act.wait_ge(q_done, 2 * n + c + 1)
                    act.activation(q_t[:, c, :], work_ps[c][0:HD, 0:GW], ACT.Identity, bias=b_qkv_sb[:, c:c + 1],
                                   scale=1.0 / SPLIT).then_inc(q_copied, 1)
                for c in range(2):
                    act.wait_ge(k_done, 2 * n + c + 1)
                    act.activation(k_t[:, c, :], work_ps[c][0:HD, 0:GT], ACT.Identity, bias=b_qkv_sb[:, 2 + c:3 + c],
                                   scale=1.0 / SPLIT).then_inc(k_copied, 1)

            def copy_v(n, first):
                for j in range(PAIRS):
                    act.wait_ge(v_done, PAIRS * n + j + 1)
                    if not first:
                        act.wait_ge(att_done, PAIRS * (n - 1) + j + 1)
                    src = work_ps[j % 2][0:TOK, 0:DIM].rearrange("p (a b d) -> p a b d", b=2, d=HDIM)
                    for b in range(2):
                        act.activation(v_bd[SLOT * b:SLOT * b + TOK, 2 * j, :, b, :], src[:, :, b, :], ACT.Copy,
                                       scale=1.0 / SPLIT).then_inc(v_act, 1)

            def exps(g, p):
                act.wait_ge(shift_done, PAIRS * g + p + 1)
                act.activation(prob[p % 2][:, :, 0:TOK], shifted[p % 2][:], ACT.Exp).then_inc(exp_done, 1)

            def copy_prob(g, p):
                for s in range(2):
                    act.wait_ge(prob_turned, 2 * (PAIRS * g + p) + s + 1)
                    src = turn_ps[s][:, 0:384].rearrange("p (a i t) -> p a i t", a=3, i=2)[:, :, :, 0:TOK]
                    act.activation(prob_t[:, 3 * s:3 * s + 3, :, :], src, ACT.Copy).then_inc(prob_copied, 1)

            def copy_att(g):
                act.wait_ge(att_done, PAIRS * g + PAIRS)
                for c in range(2):
                    act.activation(att_t[:, c, 0:GT], att_ps[c][0:HD, 0:GT], ACT.Identity,
                                   bias=b_qkv_sb[:, 4 + c:5 + c]).then_inc(att_copied, 1)

            def copy_high2(n):
                for c in range(2):
                    act.wait_ge(xn_turned[1], 2 * n + c + 1)
                    act.activation(xs[:, c, at(n * GT, GT)], work_ps[c][0:HD, 0:GT], ACT.Copy).then_inc(xt_high[1], 1)

            def split_high(g):
                act.activation(w1_hl[:, 0, at(g * SLICE1, SLICE1)], w1_sb[:, at(g * SLICE1, SLICE1)], ACT.Copy,
                               scale=SPLIT).then_inc(w_high, 1)
                act.activation(w2_hl[:, 0, at(g * SLICE2, SLICE2)], w2_sb[:, at(g * SLICE2, SLICE2)], ACT.Copy,
                               scale=SPLIT).then_inc(w_high, 1)

            def group(g, first, last):
                exps(g, 0)
                copy_prob(g, 0)
                exps(g, 1)
                if not first:
                    copy_high2(g - 1)
                copy_prob(g, 1)
                exps(g, 2)
                split_high(g)
                if not last:
                    copy_halves(g + 1)
                copy_prob(g, 2)
                exps(g, 3)
                if not last:
                    copy_qk(g + 1)
                copy_prob(g, 3)
                if not last:
                    copy_v(g + 1, False)
                copy_att(g)

            act.wait_ge(qkv_full, 4)
            act.activation(qkv_hl[:, 0, :, :], w_in_sb[:], ACT.Copy, scale=SPLIT).then_inc(qkv_high, 1)
            copy_halves(0)
            copy_qk(0)
            act.wait_ge(zeroed, 7)
            copy_v(0, True)
            act.wait_ge(expert_loaded, 16 * 7)
            group(0, True, False)
            with act.Fori(1, NG - 1) as g:
                group(g, False, False)
            group(NG - 1, False, True)
            copy_high2(NG - 1)

            act.wait_ge(routing, 3)
            act.activation(score_e[:], logit_s[:], ACT.Exp).then_inc(scores_exp, 1)

            act.wait_ge(places_ready, 2)
            act.wait_ge(xt_low[1], 2 * NG)
            with act.Fori(0, IMAGES // 4) as b:
                for k in (1, 3):
                    to = act.value_load(place_i[0:1, at(b * 4 + k, 1)], min_val=0, max_val=(BLOCKS * BI - 1) * TOK)
                    act.activation(x_sorted[:, :, at(to, TOK)], xs[:, :, at((b * 4 + k) * TOK, TOK)], ACT.Copy)\
                        .then_inc(sorted_act, 1)

            def gelu(j, e, first):
                for m in range(FM):
                    act.wait_ge(hid_done, j * FM + m + 1)
                    if not (first and m < 2):
                        act.wait_ge(hid_low, j * FM + (m - 1))
                    act.activation(hid[m % 2][:], gelu_ps[m][:, 0:BW], ACT.Gelu, bias=b1_sb[:, at(e * FM + m, 1)],
                                   scale=1.0 / SPLIT).then_inc(gelu_done, 1)

            def copy_y(j, e):
                for c in range(2):
                    act.wait_ge(y_done, j * 2 + c + 1)
                    act.activation(y_sorted[:, c, at(j * BW, BW)], y_ps[c][0:HD, 0:BW], ACT.Identity,
                                   bias=b2_sb[:, at(e * 2 + c, 1)], scale=1.0 / SPLIT).then_inc(y_copied, 1)

            def expert_of(j):
                return act.value_load(expert_i[0:1, at(j, 1)], min_val=0, max_val=EXPERTS - 1)

            gelu(0, expert_of(0), True)
            with act.Fori(1, BLOCKS) as j:
                gelu(j, expert_of(j), False)
                copy_y(j - 1, expert_of(j - 1))
            copy_y(BLOCKS - 1, expert_of(BLOCKS - 1))

            for c in range(2):
                act.wait_ge(y_copied, 2 * BLOCKS)
            for t in range(NG * TILES):
                b = t // TILES * GI + t % TILES * TI
                if t >= 3:
                    act.wait_ge(y_turned, t - 2)
                of = act.value_load(place_i[0:1, b:b + 1], min_val=0, max_val=(BLOCKS * BI - 1) * TOK)
                act.activation(y_tile[t % 3][:, :, 0:TOK], y_sorted[:, :, at(of, TOK)], ACT.Copy)\
                    .then_inc(picked_act, 1)

        @block.tensor
        def _(pe):
            def embed(n, f0_free, f1_free):
                pe.wait_ge(x_loaded, n * 16 + 16)
                for t in range(TILES):
                    if t == 0:
                        pe.wait_ge(*f0_free)
                    if t == 2:
                        pe.wait_ge(*f1_free)
                    for k in range(PK):
                        mm = pe.matmul(work_ps[t // 2][0:TT, t % 2 * DIM:(t % 2 + 1) * DIM],
                                       x_sb[:, k, t * TT:(t + 1) * TT], tok_w_sb[:, k, :],
                                       start=(k == 0), stop=(k == PK - 1))
                    if t:
                        mm.then_inc(embedded, 1)

            def turn(n, w, frees):
                pe.wait_ge(xn_ready[w], n * TILES + TILES)
                for s, v in frees:
                    pe.wait_ge(s, v)
                for c in range(2):
                    for t in range(TILES):
                        mm = pe.transpose(work_ps[c][0:HD, t * TT:(t + 1) * TT], xn[w][:, t, c * HD:(c + 1) * HD],
                                          ident32_sb[0:TT, 0:TT])
                    mm.then_inc(xn_turned[w], 1)

            def qk(n):
                pe.wait_ge(xt_low[0], n * 2 + 2)
                pe.wait_ge(xt_high[0], n * 2 + 2)
                for o, cols, done in ((0, GW, q_done), (DIM, GT, k_done)):
                    for c in range(2):
                        if o:
                            pe.wait_ge(q_copied, n * 2 + c + 1)
                        i = 0
                        for kc in range(2):
                            for wh, xh in ((0, 0), (0, 1), (1, 0)):
                                mm = pe.matmul(work_ps[c][0:HD, 0:cols],
                                               qkv_hl[:, wh, kc, o + c * HD:o + (c + 1) * HD],
                                               xn_t[:, xh, kc, 0:cols], start=(i == 0), stop=(i == 5))
                                i += 1
                        mm.then_inc(done, 1)

            def values(n):
                for j in range(PAIRS):
                    if j < 2:
                        pe.wait_ge(k_copied, n * 2 + j + 1)
                    else:
                        pe.wait_ge(v_act, n * 2 * PAIRS + 2 * (j - 2) + 2)
                        pe.wait_ge(v_dve, n * 2 * PAIRS + 2 * (j - 2) + 2)
                    for b in range(2):
                        t0 = (2 * j + b) * TOK
                        i = 0
                        for kc in range(2):
                            for wh, xh in ((0, 0), (0, 1), (1, 0)):
                                mm = pe.matmul(work_ps[j % 2][SLOT * b:SLOT * b + SLOT, 0:DIM],
                                               xn_t[:, xh, kc, t0:t0 + SLOT], qkv_hl[:, wh, kc, 2 * DIM:3 * DIM],
                                               start=(i == 0), stop=(i == 5))
                                i += 1
                    mm.then_inc(v_done, 1)

            def scores(g, p, first):
                if p == 0:
                    for s in (k_spread_dve, k_spread_pool, q_copied):
                        pe.wait_ge(s, g * 2 + 2)
                if not (first and p < 2):
                    pe.wait_ge(shift_done, g * PAIRS + (p - 1))
                s = score_ps[p % 2]
                pe.matmul(s[:, 0:HEADS * TOK], ident16_sb[:], causal_sb[:], start=True, stop=True)
                for i in range(2):
                    im = 2 * p + i
                    for c in range(2):
                        mm = pe.matmul(s[SLOT * i:SLOT * i + SLOT, c * HP * TOK:(c + 1) * HP * TOK],
                                       q_t[:, c, im * TOK:im * TOK + SLOT], k_x[:, c, im, :, :],
                                       start=False, stop=True, skip_group_check=True)
                mm.then_inc(scored, 1)

            def turn_prob(g, p, first):
                pe.wait_ge(prob_ready, g * PAIRS + p + 1)
                for s in range(2):
                    if not (first and p == 0):
                        pe.wait_ge(prob_copied, (g * PAIRS + p - 1) * 2 + s + 1)
                    for a in range(3):
                        i = 3 * s + a
                        mm = pe.transpose(turn_ps[s][:, a * 128:(a + 1) * 128], prob[p % 2][:, 2 * i:2 * i + 2, :],
                                          ident32_sb[:])
                    mm.then_inc(prob_turned, 1)

            def weigh(g, p, first):
                pe.wait_ge(prob_copied, (g * PAIRS + p) * 2 + 2)
                if p == 0:
                    pe.wait_ge(v_act, g * 2 * PAIRS + 2 * PAIRS)
                    pe.wait_ge(v_dve, g * 2 * PAIRS + 2 * PAIRS)
                    if not first:
                        pe.wait_ge(att_copied, g * 2)
                for i in range(2):
                    im = 2 * p + i
                    for a in range(HP):
                        r = 32 * (a % 3)
                        mm = pe.matmul(att_ps[a // 3][r:r + 32, im * TOK:(im + 1) * TOK],
                                       v_bd[:, im, a, :, :], prob_t[:, a, i, :], start=True, stop=True)
                mm.then_inc(att_done, 1)

            def project(n, frees):
                pe.wait_ge(att_copied, n * 2 + 2)
                for s, v in frees:
                    pe.wait_ge(s, v)
                for t in range(TILES):
                    for c in range(2):
                        mm = pe.matmul(work_ps[t // 2][0:TT, t % 2 * DIM:(t % 2 + 1) * DIM],
                                       att_t[:, c, t * TT:(t + 1) * TT], w_out_sb[:, c, :],
                                       start=(c == 0), stop=(c == 1))
                    if t:
                        mm.then_inc(projected, 1)

            def values_out(n):
                return ((v_act, n * 2 * PAIRS + 2 * PAIRS), (v_dve, n * 2 * PAIRS + 2 * PAIRS))

            def turned_out(n):
                return ((xt_high[1], n * 2 + 2), (xt_low[1], n * 2 + 2), (token_sum, n * 2 + 2))

            def group(g, first, last):
                scores(g, 0, first)
                if not first:
                    project(g - 1, values_out(g))
                if not last:
                    if first:
                        for s, v in values_out(0):
                            pe.wait_ge(s, v)
                        embed(1, values_out(0)[0], values_out(0)[1])
                    else:
                        embed(g + 1, (h2_ready, (g - 1) * 2 + 1), (h2_ready, (g - 1) * 2 + 2))
                turn_prob(g, 0, first)
                scores(g, 1, first)
                if not first:
                    turn(g - 1, 1, ((h2_ready, g * 2),) if last else ((h_ready, (g + 1) * 2 + 2),))
                weigh(g, 0, first)
                turn_prob(g, 1, first)
                scores(g, 2, first)
                if not last:
                    turn(g + 1, 0, () if first else turned_out(g - 1))
                weigh(g, 1, first)
                turn_prob(g, 2, first)
                scores(g, 3, first)
                if not last:
                    qk(g + 1)
                weigh(g, 2, first)
                turn_prob(g, 3, first)
                if not last:
                    values(g + 1)
                weigh(g, 3, first)

            pe.wait_ge(attn_loaded, 16 * ATTN_LOADS)
            for kc in range(2):
                for s in range(2):
                    pe.matmul([work_ps, score_ps][kc][s][0:HD, 0:288], lora_in_sb[:, kc * HD:(kc + 1) * HD],
                              lora_in_sb[:, DIM + s * 288:DIM + (s + 1) * 288], start=True, stop=True)\
                        .then_inc(lora_done, 1)
            for kc in range(2):
                pe.matmul(turn_ps[kc][0:HD, 0:DIM], lora_out_sb[:, kc * HD:(kc + 1) * HD],
                          lora_out_sb[:, DIM:2 * DIM], start=True, stop=True).then_inc(lora_done, 1)
            pe.wait_ge(zeroed, 7)
            embed(0, (qkv_full, 4), (qkv_full, 4))
            turn(0, 0, ())
            pe.wait_ge(qkv_high, 1)
            pe.wait_ge(qkv_low, 1)
            qk(0)
            values(0)
            pe.wait_ge(out_full, 2)
            pe.wait_ge(mask_ready, 2)
            group(0, True, False)
            with pe.Fori(1, NG - 1) as g:
                group(g, False, False)
            group(NG - 1, False, True)
            project(NG - 1, turned_out(NG - 2))
            turn(NG - 1, 1, ((h2_ready, NG * 2),))

            pe.wait_ge(token_sum, 2 * NG)
            for c in range(2):
                mm = pe.matmul(score_ps[0][0:IMAGES, 0:EXPERTS], x_sum[:, c, :], wg_sb[:, c, :],
                               start=(c == 0), stop=(c == 1))
            mm.then_inc(logits_done, 1)
            pe.wait_ge(routing, 8)
            pe.wait_ge(expert_loaded, 16 * 7)
            pe.matmul(score_ps[1][0:IMAGES, 0:EXPERTS], order_sb[:, 0:IMAGES], chosen[:], start=True, stop=True)
            pe.matmul(score_ps[1][0:IMAGES, EXPERTS:2 * EXPERTS], order_sb[:, IMAGES:2 * IMAGES], chosen[:],
                      start=True, stop=True).then_inc(ranked, 1)
            pe.wait_ge(placed, 1)
            pe.matmul(turn_ps[0][0:1, 0:IMAGES], place[:], ident32_sb[0:IMAGES, 0:IMAGES], start=True, stop=True)\
                .then_inc(gates_spread, 1)
            pe.matmul(turn_ps[1][0:TT, 0:NG * TILES], slot_sel_sb[:], gate_tile[:], start=True, stop=True)\
                .then_inc(gates_spread, 1)

            def expert_of(j):
                return pe.value_load(expert_i[0:1, at(j, 1)], min_val=0, max_val=EXPERTS - 1)

            def hidden(j, e, m, first):
                if not first:
                    pe.wait_ge(gelu_done, j * FM + (m + 1 - FM))
                i = 0
                for kc in range(2):
                    for wh, xh in ((0, 0), (0, 1), (1, 0)):
                        mm = pe.matmul(gelu_ps[m][:, 0:BW],
                                       w1_hl[:, wh, at(e * (2 * FFN) + (kc * FFN + m * 128), 128)],
                                       x_sorted[:, 2 * xh + kc, at(j * BW, BW)], start=(i == 0), stop=(i == 5))
                        i += 1
                mm.then_inc(hid_done, 1)

            def outputs(j, e, par, m, first):
                pe.wait_ge(hid_high, j * FM + (m + 1))
                pe.wait_ge(hid_low, j * FM + (m + 1))
                for c in range(2):
                    if m == 0 and not first:
                        pe.wait_ge(y_copied, j * 2 + c - 1)
                    for i, (wh, xh) in enumerate(((0, 0), (0, 1), (1, 0))):
                        mm = pe.matmul(y_ps[c][0:HD, 0:BW],
                                       w2_hl[:, wh, at(e * (FM * DIM) + (m * DIM + c * HD), HD)],
                                       hid_hl[:, par, xh, m, :] if isinstance(par, int) else
                                       hid_hl[:, at(par, 1), xh, m, :].rearrange("p a t -> p (a t)"),
                                       start=(m == 0 and i == 0), stop=(m == FM - 1 and i == 2),
                                       skip_group_check=True)
                    if m == FM - 1:
                        mm.then_inc(y_done, 1)

            pe.wait_ge(places_ready, 2)
            pe.wait_ge(gates_ready, 1)
            pe.wait_ge(sorted_dve, IMAGES // 2)
            pe.wait_ge(sorted_act, IMAGES // 2)
            pe.wait_ge(w_low, 2 * NG)
            pe.wait_ge(w_high, 2 * NG)
            e = expert_of(0)
            for m in range(FM):
                hidden(0, e, m, True)
            e1, e0 = expert_of(1), expert_of(0)
            for m in range(FM):
                hidden(1, e1, m, False)
                outputs(0, e0, 0, m, True)
            with pe.Fori(2, BLOCKS) as j:
                e1, e0 = expert_of(j), expert_of(j - 1)
                par = pe.snap((j - 1) & 1)
                for m in range(FM):
                    hidden(j, e1, m, False)
                    outputs(j - 1, e0, par, m, False)
            e0 = expert_of(BLOCKS - 1)
            for m in range(FM):
                outputs(BLOCKS - 1, e0, (BLOCKS - 1) % 2, m, False)

            for t in range(NG * TILES):
                pe.wait_ge(picked_act, t + 1)
                pe.wait_ge(picked_dve, t + 1)
                if t >= 2:
                    pe.wait_ge(out_ready, t - 1)
                for c in range(2):
                    mm = pe.transpose(work_ps[t % 2][0:TT, c * HD:(c + 1) * HD], y_tile[t % 3][:, c, :],
                                      ident32_sb[0:HD, 0:HD])
                mm.then_inc(y_turned, 1)

        @block.vector
        def _(dve):
            def add_positions(n):
                dve.wait_ge(embedded, n * 2 + 1)
                dve.tensor_tensor(h[:, at(n * TILES, 2), :],
                                  work_ps[0][0:TT, 0:2 * DIM].rearrange("p (a d) -> p a d", a=2),
                                  pos_sb[:].unsqueeze(1).broadcast_to([TT, 2, DIM]), ALU.add).then_inc(h_ready, 1)
                dve.wait_ge(embedded, n * 2 + 2)
                dve.tensor_tensor(h[:, at(n * TILES + 2, 1), :], work_ps[1][0:TT, 0:DIM].unsqueeze(1),
                                  pos_sb[:].unsqueeze(1), ALU.add).then_inc(h_ready, 1)

            def add_attention(n):
                dve.wait_ge(bias_added, n + 1)
                dve.wait_ge(projected, n * 2 + 1)
                dve.tensor_tensor(h[:, at(n * TILES, 2), :],
                                  work_ps[0][0:TT, 0:2 * DIM].rearrange("p (a d) -> p a d", a=2),
                                  h[:, at(n * TILES, 2), :], ALU.add).then_inc(h2_ready, 1)
                dve.wait_ge(projected, n * 2 + 2)
                dve.tensor_tensor(h[:, at(n * TILES + 2, 1), :], work_ps[1][0:TT, 0:DIM].unsqueeze(1),
                                  h[:, at(n * TILES + 2, 1), :], ALU.add).then_inc(h2_ready, 1)

            def moments(n, w):
                dve.wait_ge(attn_loaded, 16 * ATTN_LOADS)
                dve.wait_ge((h_ready, h2_ready)[w], n * 2 + 2)
                for t in range(TILES):
                    dve.bn_stats(stats[w][:, t, :], h[:, at(n * TILES + t, 1), :].rearrange("p a d -> p (a d)"))\
                        .then_inc(stats_done[w], 1)
                dve.wait_ge(stats_done[w], n * TILES + TILES)

            def aggregate(w):
                for t in range(TILES):
                    dve.bn_aggr(mean_var[w][:, t, :], stats[w][:, t, :]).then_inc(aggr_done[w], 1)

            def norm(n, w, first):
                dve.wait_ge(rstd_done[w], n + 1)
                if not first:
                    dve.wait_ge(xn_turned[w], n * 2)
                for t in range(TILES):
                    dve.tensor_scalar(xn[w][:, t, :], h[:, at(n * TILES + t, 1), :].rearrange("p a d -> p (a d)"),
                                      mean_var[w][:, t, 0:1], rstd[w][:, t:t + 1], ALU.subtract, ALU.mult)\
                        .then_inc(xn_ready[w], 1)

            def low_halves(n):
                for c in range(2):
                    dve.wait_ge(xt_high[0], n * 2 + c + 1)
                    dve.tensor_tensor(xn_t[:, 1, c, :], work_ps[c][0:HD, 0:GW], xn_t[:, 0, c, :], ALU.subtract)\
                        .then_inc(xt_low[0], 1)

            def low_halves2(n):
                for c in range(2):
                    dve.wait_ge(xt_high[1], n * 2 + c + 1)
                    dve.tensor_tensor(xs[:, 2 + c, at(n * GT, GT)], work_ps[c][0:HD, 0:GT], xs[:, c, at(n * GT, GT)],
                                      ALU.subtract).then_inc(xt_low[1], 1)
                    dve.tensor_reduce(x_sum[:, c, at(n * GI, GI)],
                                      work_ps[c][0:HD, 0:GT].rearrange("p (i k) -> p i k", k=TOK), AX, ALU.add)\
                        .then_inc(token_sum, 1)

            def spread_keys(n):
                for c in range(2):
                    dve.wait_ge(k_copied, n * 2 + c + 1)
                    spread(dve, c, 0, POOL_HEADS).then_inc(k_spread_dve, 1)

            def copy_v(n, first):
                for j in range(PAIRS):
                    dve.wait_ge(v_act, n * 2 * PAIRS + 2 * j + 2)
                    if not first:
                        dve.wait_ge(att_done, PAIRS * (n - 1) + j + 1)
                    src = work_ps[j % 2][SLOT:SLOT + TOK, 0:DIM].rearrange("p (a b d) -> p a b d", b=2, d=HDIM)
                    for b in range(2):
                        dve.tensor_scalar(v_bd[SLOT * b:SLOT * b + TOK, 2 * j + 1, :, b, :], src[:, :, b, :],
                                          1.0 / SPLIT, None, ALU.mult).then_inc(v_dve, 1)

            def shift(g, p, first):
                s = score_ps[p % 2][:, 0:HEADS * TOK].rearrange("p (a k) -> p a k", k=TOK)
                dve.wait_ge(scored, g * PAIRS + p + 1)
                dve.tensor_reduce(row_max[p % 2][:], s, AX, ALU.max).then_inc(max_done, 1)
                dve.wait_ge(max_done, g * PAIRS + p + 1)
                if not (first and p < 2):
                    dve.wait_ge(exp_done, g * PAIRS + (p - 1))
                dve.tensor_tensor(shifted[p % 2][:], s,
                                  row_max[p % 2][:].unsqueeze(2).broadcast_to([128, HEADS, TOK]), ALU.subtract)\
                    .then_inc(shift_done, 1)

            def sums(g, p, first):
                dve.wait_ge(exp_done, g * PAIRS + p + 1)
                dve.tensor_reduce(row_sum[p % 2][:], prob[p % 2][:, :, 0:TOK], AX, ALU.add).then_inc(sum_done, 1)
                dve.wait_ge(sum_done, g * PAIRS + p + 1)
                if not (first and p < 2):
                    dve.wait_ge(prob_ready, g * PAIRS + (p - 1))
                dve.reciprocal(inv_sum[p % 2][:], row_sum[p % 2][:]).then_inc(inv_done, 1)

            def split_low(g):
                dve.wait_ge(w_high, g * 2 + 2)
                for hl, w, n in ((w1_hl, w1_sb, SLICE1), (w2_hl, w2_sb, SLICE2)):
                    dve.scalar_tensor_tensor(out=hl[:, 1, at(g * n, n)], in0=w[:, at(g * n, n)], scalar=SPLIT,
                                             in1=hl[:, 0, at(g * n, n)], op0=ALU.mult, op1=ALU.subtract)\
                        .then_inc(w_low, 1)

            def group(g, first, last):
                shift(g, 0, first)
                if not first:
                    add_attention(g - 1)
                    moments(g - 1, 1)
                sums(g, 0, first)
                if not first:
                    aggregate(1)
                if not last:
                    add_positions(g + 1)
                    moments(g + 1, 0)
                if not first:
                    norm(g - 1, 1, False)
                if not last:
                    aggregate(0)
                shift(g, 1, first)
                if not last:
                    norm(g + 1, 0, False)
                sums(g, 1, first)
                if not first:
                    low_halves2(g - 1)
                shift(g, 2, first)
                sums(g, 2, first)
                if not last:
                    low_halves(g + 1)
                shift(g, 3, first)
                split_low(g)
                sums(g, 3, first)
                if not last:
                    spread_keys(g + 1)
                    copy_v(g + 1, False)

            dve.wait_ge(lora_done, 6)
            dve.wait_ge(attn_loaded, 16 * ATTN_LOADS)
            for kc in range(2):
                for s in range(2):
                    w = w_in_sb[:, kc, s * 288:(s + 1) * 288]
                    dve.scalar_tensor_tensor(out=w, in0=[work_ps, score_ps][kc][s][0:HD, 0:288], scalar=LORA, in1=w,
                                             op0=ALU.mult, op1=ALU.add).then_inc(qkv_full, 1)
            for kc in range(2):
                w = w_out_sb[:, kc, :]
                dve.scalar_tensor_tensor(out=w, in0=turn_ps[kc][0:HD, 0:DIM], scalar=LORA, in1=w,
                                         op0=ALU.mult, op1=ALU.add).then_inc(out_full, 1)
            dve.wait_ge(qkv_high, 1)
            dve.wait_ge(pos_added, 1)
            add_positions(0)
            moments(0, 0)
            aggregate(0)
            dve.scalar_tensor_tensor(out=qkv_hl[:, 1, :, :], in0=w_in_sb[:], scalar=SPLIT, in1=qkv_hl[:, 0, :, :],
                                     op0=ALU.mult, op1=ALU.subtract).then_inc(qkv_low, 1)
            norm(0, 0, True)
            low_halves(0)
            spread_keys(0)
            dve.wait_ge(zeroed, 7)
            copy_v(0, True)
            group(0, True, False)
            with dve.Fori(1, NG - 1) as g:
                group(g, False, False)
            group(NG - 1, False, True)
            add_attention(NG - 1)
            moments(NG - 1, 1)
            aggregate(1)
            norm(NG - 1, 1, False)
            low_halves2(NG - 1)

            step = 0

            def then(ins):
                nonlocal step
                step += 1
                ins.then_inc(routing, 1)
                dve.wait_ge(routing, step)

            dve.wait_ge(logits_done, 1)
            then(dve.tensor_scalar(logit[:], score_ps[0][0:IMAGES, 0:EXPERTS], 1.0 / TOK, None, ALU.mult))
            then(dve.tensor_reduce(top[:], logit[:], AX, ALU.max))
            then(dve.tensor_scalar(logit_s[:], logit[:], top[:], None, ALU.subtract))
            then(dve.tensor_scalar(is_top[:], logit[:], top[:], None, ALU.is_equal))
            then(dve.tensor_scalar(not_first[:], is_top[:, 0:1], -1.0, 1.0, ALU.mult, ALU.add))
            then(dve.tensor_copy(chosen[:, 0:1], is_top[:, 0:1]))
            then(dve.tensor_tensor(chosen[:, 1:2], is_top[:, 1:2], not_first[:], ALU.mult))
            then(dve.tensor_tensor(chosen[:, 2:3], not_first[:], chosen[:, 1:2], ALU.subtract))
            dve.wait_ge(scores_exp, 1)
            then(dve.tensor_reduce(score_s[:], score_e[:], AX, ALU.add))
            then(dve.reciprocal(gate[:], score_s[:]))
            dve.wait_ge(expert_loaded, 16 * 7)
            then(dve.tensor_scalar(gate_tile[:], tile_sel_sb[:], gate[:], None, ALU.mult))
            dve.wait_ge(ranked, 1)
            then(dve.tensor_tensor(over[:],
                                   score_ps[1][0:IMAGES, EXPERTS:2 * EXPERTS].unsqueeze(2)
                                   .broadcast_to([IMAGES, EXPERTS, ROUND]),
                                   steps_sb[:, 0:ROUND].unsqueeze(1).broadcast_to([IMAGES, EXPERTS, ROUND]),
                                   ALU.is_gt))
            then(dve.tensor_reduce(n_block[:], over[:], AX, ALU.add))
            then(dve.memset(start[:, 0:1], 0.0))
            then(dve.tensor_copy(start[:, 1:2], n_block[:, 0:1]))
            then(dve.tensor_tensor(start[:, 2:3], n_block[:, 0:1], n_block[:, 1:2], ALU.add))
            then(dve.scalar_tensor_tensor(out=place_e[:], in0=start[:], scalar=float(BI),
                                          in1=score_ps[1][0:IMAGES, 0:EXPERTS], op0=ALU.mult, op1=ALU.add))
            then(dve.scalar_tensor_tensor(out=place_c[:], in0=place_e[:], scalar=float(TOK), in1=chosen[:],
                                          op0=ALU.mult, op1=ALU.mult))
            dve.tensor_reduce(place[:], place_c[:], AX, ALU.add).then_inc(placed, 1)
            for k in range(2):
                then(dve.tensor_scalar(begun[:, k, :], steps_sb[0:1, ROUND:], start[0:1, k + 1:k + 2], None,
                                       ALU.is_ge))
            dve.tensor_tensor(expert_i[:], begun[:, 0, :], begun[:, 1, :], ALU.add).then_inc(places_ready, 1)
            dve.wait_ge(gates_spread, 1)
            dve.tensor_copy(place_i[:], turn_ps[0][0:1, 0:IMAGES]).then_inc(places_ready, 1)
            dve.wait_ge(gates_spread, 2)
            dve.tensor_copy(gate_tok[:], turn_ps[1][0:TT, 0:NG * TILES]).then_inc(gates_ready, 1)

            dve.wait_ge(places_ready, 2)
            dve.wait_ge(zeroed, 8)
            dve.wait_ge(xt_high[1], 2 * NG)
            dve.wait_ge(xt_low[1], 2 * NG)
            with dve.Fori(0, IMAGES // 4) as b:
                for k in (0, 2):
                    to = dve.value_load(place_i[0:1, at(b * 4 + k, 1)], min_val=0, max_val=(BLOCKS * BI - 1) * TOK)
                    dve.tensor_copy(x_sorted[:, :, at(to, TOK)], xs[:, :, at((b * 4 + k) * TOK, TOK)])\
                        .then_inc(sorted_dve, 1)

            def halves(j, par, first):
                if not first:
                    dve.wait_ge(y_done, j * 2 - 2)
                for m in range(FM):
                    hh, hl = (hid_hl[:, par, k, m, :] if isinstance(par, int) else
                              hid_hl[:, at(par, 1), k, m, :].rearrange("p a t -> p (a t)") for k in range(2))
                    dve.wait_ge(gelu_done, j * FM + (m + 1))
                    dve.tensor_copy(hh, hid[m % 2][:]).then_inc(hid_high, 1)
                    dve.wait_ge(hid_high, j * FM + (m + 1))
                    dve.tensor_tensor(hl, hid[m % 2][:], hh, ALU.subtract).then_inc(hid_low, 1)

            halves(0, 0, True)
            halves(1, 1, True)
            with dve.Fori(2, BLOCKS) as j:
                par = dve.snap(j & 1)
                halves(j, par, False)

            def pick(t):
                b = t // TILES * GI + t % TILES * TI
                if t >= 3:
                    dve.wait_ge(y_turned, t - 2)
                for k in range(1, TI):
                    i = b + k if k < TAILS[t % TILES] else b
                    of = dve.value_load(place_i[0:1, i:i + 1], min_val=0, max_val=(BLOCKS * BI - 1) * TOK)
                    cp = dve.tensor_copy(y_tile[t % 3][:, :, k * TOK:(k + 1) * TOK], y_sorted[:, :, at(of, TOK)])
                cp.then_inc(picked_dve, 1)

            dve.wait_ge(y_copied, 2 * BLOCKS)
            for t in range(NG * TILES + 1):
                if t < NG * TILES:
                    pick(t)
                if t >= 1:
                    dve.wait_ge(y_turned, t)
                    if t > OUTS:
                        dve.wait_ge(stored[(t - 1) % OUTS], 16 * ((t - 1) // OUTS))
                    dve.scalar_tensor_tensor(out=out_sb[(t - 1) % OUTS], in0=work_ps[(t - 1) % 2][0:TT, 0:DIM],
                                             scalar=gate_tok[:, t - 1:t], in1=h[:, t - 1, :],
                                             op0=ALU.mult, op1=ALU.add).then_inc(out_ready, 1)


def _laid_out(x, L0_tok_W, L0_tok_b, L0_tok_cls_token, L0_tok_pos_table, L0_attn_w_in, L0_attn_b_in, L0_attn_A_in,
              L0_attn_B_in, L0_attn_w_out, L0_attn_b_out, L0_attn_A_out, L0_attn_B_out, L0_ffn_Wg, L0_ffn_W1,
              L0_ffn_b1, L0_ffn_W2, L0_ffn_b2):
    a = {k: np.asarray(v) for k, v in locals().items()}
    f = np.float32
    p = a["x"].reshape(IMAGES, GRID, PATCH, GRID, PATCH, 3).transpose(0, 1, 3, 2, 4, 5)
    p = p.reshape(IMAGES, TOK - 1, PIX)
    p = np.concatenate([np.zeros((IMAGES, 1, PIX), f), p], axis=1)
    cls = a["L0_tok_cls_token"].reshape(1, DIM)
    rows = np.concatenate([cls, np.broadcast_to(a["L0_tok_b"], (TOK - 1, DIM))], axis=0)
    b_in = a["L0_attn_b_in"].reshape(6, HD)
    image = np.arange(IMAGES)
    part = np.arange(HD)
    head_sel = (part[:, None] // HDIM == np.arange(HP)[None, :]).astype(f)
    q = np.arange(128)[:, None]
    k = np.tile(np.arange(TOK), HEADS)[None, :]
    hidden = (q % SLOT < TOK) & (k > q % SLOT)
    tile = image // GI * TILES + image % GI // TI
    slot = image % GI % TI
    steps = np.concatenate([BI * np.arange(ROUND), np.arange(BLOCKS)]).astype(f)
    return {
        "x": p.reshape(NG, GT, PK, 128).transpose(0, 3, 2, 1),
        "tok_w": a["L0_tok_W"].reshape(PK, 128, DIM).transpose(1, 0, 2),
        "row_add": np.tile(rows, (TI, 1)),
        "pos_rows": np.tile(a["L0_tok_pos_table"], (TI, 1)),
        "w_in": a["L0_attn_w_in"].reshape(2, HD, 3 * DIM).transpose(1, 0, 2),
        "lora_in": np.concatenate([a["L0_attn_B_in"].T, a["L0_attn_A_in"]], axis=1),
        "w_out": a["L0_attn_w_out"].reshape(2, HD, DIM).transpose(1, 0, 2),
        "lora_out": np.concatenate([a["L0_attn_B_out"].T, a["L0_attn_A_out"]], axis=1),
        "b_qkv": b_in.T,
        "b_out": np.tile(a["L0_attn_b_out"][None, :], (TT, 1)),
        "head_sel": head_sel,
        "causal": np.where(hidden, -1e9, 0.0).astype(f),
        "ident32": np.eye(128, dtype=f),
        "wg": a["L0_ffn_Wg"].T.reshape(2, HD, EXPERTS).transpose(1, 0, 2),
        "w1": a["L0_ffn_W1"].reshape(EXPERTS, 2, HD, FFN).transpose(2, 0, 1, 3).reshape(HD, -1),
        "b1": a["L0_ffn_b1"].reshape(EXPERTS * FM, 128).T,
        "w2": a["L0_ffn_W2"].reshape(EXPERTS, FM, 128, DIM).transpose(2, 0, 1, 3).reshape(128, -1),
        "b2": a["L0_ffn_b2"].reshape(EXPERTS * 2, HD).T,
        "order": np.concatenate([np.triu(np.ones((IMAGES, IMAGES)), 1), np.ones((IMAGES, IMAGES))], 1).astype(f),
        "tile_sel": (tile[:, None] == np.arange(NG * TILES)[None, :]).astype(f),
        "slot_sel": (slot[:, None] == np.arange(TT)[None, :] // TOK).astype(f),
        "steps": np.tile(steps[None, :], (IMAGES, 1)),
    }


def kernel(**inputs):
    import concourse.bacc as bacc
    from concourse.bass_utils import run_bass_kernel_spmd

    arrays = {k: np.ascontiguousarray(v) for k, v in _laid_out(**inputs).items()}
    nc = bacc.Bacc("TRN2", target_bir_lowering=False, num_devices=1)
    aps = {k: nc.dram_tensor(f"in_{k}", v.shape, mybir.dt.from_np(v.dtype), kind="ExternalInput").ap()
           for k, v in arrays.items()}
    out = nc.dram_tensor("out", (IMAGES * TOK, DIM), F32, kind="ExternalOutput").ap()
    vit_layer(nc, **aps, out=out)
    r = run_bass_kernel_spmd(nc, [{f"in_{k}": v for k, v in arrays.items()}], core_ids=[0])
    return r.results[0]["out"].reshape(IMAGES, TOK, DIM)
```

```python
from contextlib import ExitStack

import numpy as np

import concourse.bass as bass
from concourse import mybir

F32 = mybir.dt.float32
F16 = mybir.dt.float16
BF16 = mybir.dt.bfloat16
I32 = mybir.dt.int32
ALU = mybir.AluOpType
ACT = mybir.ActivationFunctionType
AX = mybir.AxisListType.X

IMAGES = 64
PATCH = 16
GRID = 6
TOK = GRID * GRID + 1
PIX = PATCH * PATCH * 3
PK = PIX // 128
DIM = 192
HD = DIM // 2
HEADS = 12
HDIM = DIM // HEADS
HP = HEADS // 2
FFN = 768
FM = FFN // 128
EXPERTS = 3
LORA = 8.0
EPS = 1e-5
SPLIT = 64.0

GI = 8
NG = IMAGES // GI
GT = GI * TOK
TI = 3
TT = TI * TOK
TILES = -(-GI // TI)
GW = TILES * TT
PAIRS = GI // 2
SLOT = 64

BI = 9
BW = BI * TOK
BLOCKS = (IMAGES + EXPERTS * (BI - 1)) // BI
ROUND = 8


def vit_layer(nc, x, tok_w, row_add, pos_rows, w_in, lora_in, w_out, lora_out, b_qkv, b_out, head_sel, causal,
              ident32, wg, w1, b1, w2, b2, order, tile_sel, slot_sel, steps, out):
    with ExitStack() as ctx:
        def sb(name, shape, dt=F32):
            return ctx.enter_context(nc.sbuf_tensor(name, shape, dt))

        def sem(name):
            return ctx.enter_context(nc.semaphore(name))

        at = bass.ds

        score_ps = ctx.enter_context(nc.psum_tensor("score_ps", [128, 512], F32))
        turn_ps = [ctx.enter_context(nc.psum_tensor(f"turn_ps{i}", [128, 512], F32)) for i in range(2)]
        att_ps = [ctx.enter_context(nc.psum_tensor(f"att_ps{i}", [128, 512], F32)) for i in range(2)]
        work_ps = [ctx.enter_context(nc.psum_tensor(f"work_ps{i}", [128, 512], F32)) for i in range(3)]

        gelu_ps = [score_ps, *turn_ps, *work_ps]
        y_ps = att_ps

        lora_ps = [work_ps[1], work_ps[2], score_ps, att_ps[0]]

        early = sb("early", [128, PK * GW + PK * DIM + 2 * 3 * DIM])
        x_sb = early[:, 0:PK * GW].rearrange("p (k t) -> p k t", k=PK)
        tok_w_sb = early[:, PK * GW:PK * (GW + DIM)].rearrange("p (k d) -> p k d", k=PK)
        row_add_sb = sb("row_add_sb", [TT, DIM])
        pos_sb = sb("pos_sb", [TT, DIM])
        w_in_sb = early[0:HD, PK * (GW + DIM):].rearrange("p (k d) -> p k d", k=2)
        w_out_sb = sb("w_out_sb", [HD, 2, DIM])
        qkv_hl = sb("qkv_hl", [HD, 2, 2, 3 * DIM], F16)
        b_qkv_sb = sb("b_qkv_sb", [HD, 6])
        b_out_sb = sb("b_out_sb", [TT, DIM])
        head_sel_sb = sb("head_sel_sb", [HD, HP])
        causal_sb = sb("causal_sb", [128, HEADS * TOK], BF16)
        ident16_sb = sb("ident16_sb", [128, 128], BF16)
        ident32_sb = sb("ident32_sb", [128, 128])
        wg_sb = sb("wg_sb", [HD, 2, EXPERTS])
        staged = sb("staged", [128, EXPERTS * (2 * FFN + FM * DIM)])
        w1_sb = staged[0:HD, 0:EXPERTS * 2 * FFN]
        w2_sb = staged[:, EXPERTS * 2 * FFN:]
        w1_hl = sb("w1_hl", [HD, 2, EXPERTS * 2 * FFN], F16)
        w2_hl = sb("w2_hl", [128, 2, EXPERTS * FM * DIM], F16)
        b1_sb = sb("b1_sb", [128, EXPERTS * FM])
        b2_sb = sb("b2_sb", [HD, EXPERTS * 2])
        order_sb = sb("order_sb", [IMAGES, 2 * IMAGES])
        tile_sel_sb = sb("tile_sel_sb", [IMAGES, NG * TILES])
        slot_sel_sb = sb("slot_sel_sb", [IMAGES, TT])
        steps_sb = sb("steps_sb", [IMAGES, ROUND + BLOCKS])

        h = sb("h", [TT, NG * TILES, DIM])
        stats = [sb(f"stats{i}", [TT, TILES, 6]) for i in range(2)]
        mean_var = [sb(f"mean_var{i}", [TT, TILES, 2]) for i in range(2)]
        var_eps = [sb(f"var_eps{i}", [TT, TILES]) for i in range(2)]
        rstd = [sb(f"rstd{i}", [TT, TILES]) for i in range(2)]
        neg_half = sb("neg_half", [TT, TILES])
        eps_sb = sb("eps_sb", [TT, TILES])
        xn = [sb(f"xn{i}", [TT, TILES, DIM]) for i in range(2)]
        xn_t = sb("xn_t", [HD, 2, 2, GW], F16)
        q_t = sb("q_t", [HD, 2, GW])
        k_t = sb("k_t", [HD, 2, GT])
        k_x = sb("k_x", [HD, 2, GI, HP, TOK])
        v_bd = sb("v_bd", [128, GI, HP, 2, HDIM])
        lora_in_sb = k_x[0:4, 0, 0:4, :, :].rearrange("p i a k -> p (i a k)")[:, 0:4 * DIM]
        lora_out_sb = k_x[0:4, 1, 0:4, :, :].rearrange("p i a k -> p (i a k)")[:, 0:2 * DIM]
        row_max = [sb(f"row_max{i}", [128, HEADS]) for i in range(2)]
        prob = [sb(f"prob{i}", [128, HEADS, SLOT]) for i in range(PAIRS)]
        row_sum = [sb(f"row_sum{i}", [128, HEADS]) for i in range(2)]
        inv_sum = [sb(f"inv_sum{i}", [128, HEADS]) for i in range(2)]
        prob_t = sb("prob_t", [128, HP, 2, TOK])
        att_t = sb("att_t", [HD, 2, GW])

        xs = sb("xs", [HD, 4, IMAGES * TOK], F16)
        x_sum = sb("x_sum", [HD, 2, IMAGES])
        sort_room = sb("sort_room", [128, 2 * BLOCKS * BW])
        x_sorted = sort_room[0:HD, :].bitcast(F16).rearrange("p (q t) -> p q t", q=4)
        x1_sb = sort_room[:, 0:PK * GW].rearrange("p (k t) -> p k t", k=PK)
        logit = sb("logit", [IMAGES, EXPERTS])
        top = sb("top", [IMAGES, 1])
        logit_s = sb("logit_s", [IMAGES, EXPERTS])
        score_e = sb("score_e", [IMAGES, EXPERTS])
        score_s = sb("score_s", [IMAGES, 1])
        gate = sb("gate", [IMAGES, 1])
        is_top = sb("is_top", [IMAGES, EXPERTS])
        not_first = sb("not_first", [IMAGES, 1])
        chosen = sb("chosen", [IMAGES, EXPERTS])
        over = sb("over", [IMAGES, EXPERTS, ROUND])
        n_block = sb("n_block", [IMAGES, EXPERTS])
        start = sb("start", [IMAGES, EXPERTS])
        place_e = sb("place_e", [IMAGES, EXPERTS])
        place_c = sb("place_c", [IMAGES, EXPERTS])
        place = sb("place", [IMAGES, 1])
        gate_tile = sb("gate_tile", [IMAGES, NG * TILES])
        gate_tok = sb("gate_tok", [TT, NG * TILES])
        begun = sb("begun", [1, 2, BLOCKS])
        place_i = sb("place_i", [1, IMAGES], I32)
        expert_i = sb("expert_i", [1, BLOCKS], I32)
        hid = [sb(f"hid{i}", [128, BW]) for i in range(2)]
        hid_hl = early[:, 0:2 * FM * BW].bitcast(F16)\
            .rearrange("p (b k m t) -> p b k m t", b=2, k=2, m=FM)
        y_sorted = staged[0:HD, 0:2 * BLOCKS * BW].rearrange("p (c t) -> p c t", c=2)
        q_flat = q_t[:].rearrange("p c t -> p (c t)")
        y_tile = [q_flat[:, i * 2 * TT:(i + 1) * 2 * TT].rearrange("p (c t) -> p c t", c=2) for i in range(3)]
        out_sb = [xn[i][:, t, :] for i in range(2) for t in range(TILES)]
        OUTS = len(out_sb)

        x_loaded = sem("x_loaded")
        x1_loaded = sem("x1_loaded")
        embed_loaded = sem("embed_loaded")
        attn_loaded = sem("attn_loaded")
        lora_loaded = sem("lora_loaded")
        expert_loaded = sem("expert_loaded")
        zeroed = sem("zeroed")
        pos_added = sem("pos_added")
        mask_ready = sem("mask_ready")
        lora_done = sem("lora_done")
        qkv_full = sem("qkv_full")
        qkv_high = sem("qkv_high")
        qkv_low = sem("qkv_low")
        out_full = sem("out_full")
        embedded = sem("embedded")
        h_ready = sem("h_ready")
        stats_done = [sem(f"stats_done{i}") for i in range(2)]
        aggr_done = [sem(f"aggr_done{i}") for i in range(2)]
        eps_added = [sem(f"eps_added{i}") for i in range(2)]
        rstd_done = [sem(f"rstd_done{i}") for i in range(2)]
        xn_ready = [sem(f"xn_ready{i}") for i in range(2)]
        xn_turned = [sem(f"xn_turned{i}") for i in range(2)]
        xt_high = [sem(f"xt_high{i}") for i in range(2)]
        xt_low = [sem(f"xt_low{i}") for i in range(2)]
        token_sum = sem("token_sum")
        bias_added = sem("bias_added")
        q_done = sem("q_done")
        q_copied = sem("q_copied")
        k_done = sem("k_done")
        k_copied = sem("k_copied")
        k_spread_dve = sem("k_spread_dve")
        k_spread_pool = sem("k_spread_pool")
        v_done = sem("v_done")
        v_act = sem("v_act")
        v_dve = sem("v_dve")
        scored = sem("scored")
        max_done = sem("max_done")
        shift_done = sem("shift_done")
        exp_done = sem("exp_done")
        sum_done = sem("sum_done")
        inv_done = sem("inv_done")
        prob_ready = sem("prob_ready")
        prob_turned = sem("prob_turned")
        prob_copied = sem("prob_copied")
        att_done = sem("att_done")
        att_copied = sem("att_copied")
        projected = sem("projected")
        h2_ready = sem("h2_ready")
        w_scaled = sem("w_scaled")
        w_high = sem("w_high")
        w_low = sem("w_low")
        logits_done = sem("logits_done")
        routing = sem("routing")
        scores_exp = sem("scores_exp")
        ranked = sem("ranked")
        placed = sem("placed")
        gates_spread = sem("gates_spread")
        gates_ready = sem("gates_ready")
        places_ready = sem("places_ready")
        sorted_dve = sem("sorted_dve")
        sorted_act = sem("sorted_act")
        hid_done = sem("hid_done")
        gelu_done = sem("gelu_done")
        hid_high = sem("hid_high")
        hid_low = sem("hid_low")
        y_done = sem("y_done")
        y_copied = sem("y_copied")
        picked_act = sem("picked_act")
        picked_dve = sem("picked_dve")
        y_turned = sem("y_turned")
        out_ready = sem("out_ready")
        stored = [sem(f"stored{i}") for i in range(2 * TILES)]

        block = ctx.enter_context(nc.Block())
        ATTN_LOADS = 5
        V_BANK = (1, 2, 0, 1)
        POOL_HEADS = 3
        EXPERT_LOADS = 9
        SLICE1 = EXPERTS * 2 * FFN // NG
        SLICE2 = EXPERTS * FM * DIM // NG
        TAILS = [GI - TI * t if GI < TI * (t + 1) else TI for t in range(TILES)]

        def spread(eng, c, a, b):
            n = b - a
            return eng.tensor_tensor(k_x[:, c, :, a:b, :],
                                     k_t[:, c, :].rearrange("p (i k) -> p i k", k=TOK).unsqueeze(2)
                                     .broadcast_to([HD, GI, n, TOK]),
                                     head_sel_sb[:, a:b].unsqueeze(1).unsqueeze(3).broadcast_to([HD, GI, n, TOK]),
                                     ALU.mult)

        def places(eng, regs, first):
            eng.load(regs, place_i[0:1, at(first, len(regs))])
            return [eng.snap(reg, min_val=0, max_val=(BLOCKS * BI - 1) * TOK) for reg in regs]

        def is_first(g):
            return isinstance(g, int) and g == 0

        def is_late(g):
            return isinstance(g, int) and g >= NG - 2

        def is_last(g):
            return isinstance(g, int) and g == NG - 1

        @block.sync
        def _(sp):
            sp.dma_start(tok_w_sb[:], tok_w).then_inc(embed_loaded, 16)
            sp.dma_start(x_sb[:, :, 0:GT], x[0]).then_inc(x_loaded, 16)
            for dst, src in ((lora_in_sb, lora_in), (w_in_sb, w_in), (w_out_sb, w_out), (lora_out_sb, lora_out)):
                sp.dma_start(dst[:], src).then_inc(lora_loaded, 16)
            sp.dma_start(x1_sb[:, :, 0:GT], x[1]).then_inc(x1_loaded, 16)
            sp.dma_start(w1_sb[:], w1).then_inc(expert_loaded, 16)
            sp.wait_ge(embedded, 2)
            sp.dma_start(x_sb[:, :, 0:GT], x[2]).then_inc(x_loaded, 16)
            for dst, src in ((w2_sb, w2), (b1_sb, b1), (b2_sb, b2), (tile_sel_sb, tile_sel),
                             (slot_sel_sb, slot_sel), (steps_sb, steps), (wg_sb, wg), (order_sb, order)):
                sp.dma_start(dst[:], src).then_inc(expert_loaded, 16)
            with sp.Fori(3, NG) as g:
                sp.wait_ge(embedded, g * 2)
                sp.dma_start(x_sb[:, :, 0:GT], x[at(g, 1)].rearrange("a p k t -> (a p) k t")).then_inc(x_loaded, 16)
            for t in range(NG * TILES):
                n = TAILS[t % TILES] * TOK
                row = (t // TILES * GI + t % TILES * TI) * TOK
                sp.wait_ge(out_ready, t + 1)
                sp.dma_start(out[row:row + n, :], out_sb[t % OUTS][0:n, :]).then_inc(stored[t % OUTS], 16)
            for i in range(OUTS):
                sp.wait_ge(stored[i], 16 * (NG * TILES // OUTS))

        @block.gpsimd
        def _(pool):
            pool.memset(x_sb[:, :, GT:GW], 0.0).then_inc(zeroed, 1)
            pool.memset(x1_sb[:, :, GT:GW], 0.0).then_inc(zeroed, 1)
            pool.memset(neg_half[:], -0.5).then_inc(zeroed, 1)
            pool.memset(eps_sb[:], EPS).then_inc(zeroed, 1)
            pool.memset(v_bd[:], 0.0).then_inc(zeroed, 1)
            for i in range(PAIRS):
                pool.memset(prob[i][:], 0.0).then_inc(zeroed, 1)
            pool.memset(att_t[:, :, GT:GW], 0.0).then_inc(zeroed, 1)
            pool.wait_ge(embed_loaded, 16 * 3)
            pool.tensor_tensor(pos_sb[:], pos_sb[:], row_add_sb[:], ALU.add).then_inc(pos_added, 1)
            pool.wait_ge(attn_loaded, 16 * ATTN_LOADS)
            pool.tensor_copy(causal_sb[:], prob_t[:].rearrange("p a i k -> p (a i k)")).then_inc(mask_ready, 1)
            pool.tensor_copy(ident16_sb[:], ident32_sb[:]).then_inc(mask_ready, 1)

            def inverse_std(n, w):
                pool.wait_ge(aggr_done[w], TILES * n + TILES)
                pool.tensor_tensor(var_eps[w][:], mean_var[w][:, :, 1], eps_sb[:], ALU.add).then_inc(eps_added[w], 1)
                pool.wait_ge(eps_added[w], n + 1)
                pool.tensor_tensor(rstd[w][:], var_eps[w][:], neg_half[:], ALU.pow).then_inc(rstd_done[w], 1)

            def normalise(g, p):
                pool.wait_ge(inv_done, PAIRS * g + p + 1)
                pr = prob[p][:, :, 0:TOK]
                pool.tensor_tensor(pr, pr, inv_sum[p % 2][:].unsqueeze(2).broadcast_to([128, HEADS, TOK]),
                                   ALU.mult).then_inc(prob_ready, 1)

            def split_low(g):
                pool.wait_ge(w_high, g * 2 + 2)
                for hl, w, n in ((w1_hl, w1_sb, SLICE1), (w2_hl, w2_sb, SLICE2)):
                    pool.tensor_tensor(hl[:, 1, at(g * n, n)], w[:, at(g * n, n)], hl[:, 0, at(g * n, n)],
                                       ALU.subtract).then_inc(w_low, 1)

            def add_out_bias(n):
                pool.wait_ge(xn_ready[0], TILES * n + TILES)
                ht = h[:, at(n * TILES, TILES), :]
                pool.tensor_tensor(ht, ht, b_out_sb[:].unsqueeze(1).broadcast_to([TT, TILES, DIM]), ALU.add)\
                    .then_inc(bias_added, 1)

            def spread_keys(n):
                for c in range(2):
                    pool.wait_ge(k_copied, n * 2 + c + 1)
                    spread(pool, c, POOL_HEADS, HP).then_inc(k_spread_pool, 1)

            def group(g):
                normalise(g, 0)
                normalise(g, 1)
                if not is_first(g):
                    inverse_std(g - 1, 1)
                if not is_late(g):
                    inverse_std(g + 2, 0)
                normalise(g, 2)
                if not is_last(g):
                    spread_keys(g + 1)
                normalise(g, 3)
                if not is_late(g):
                    add_out_bias(g + 2)
                split_low(g)

            inverse_std(0, 0)
            add_out_bias(0)
            inverse_std(1, 0)
            spread_keys(0)
            add_out_bias(1)
            pool.wait_ge(embedded, 4)
            pool.memset(sort_room[0:HD, 0:PK * GW], 0.0).then_inc(zeroed, 1)
            pool.wait_ge(zeroed, 12)
            group(0)
            group(1)
            with pool.Fori(2, NG - 2) as g:
                group(g)
            group(NG - 2)
            group(NG - 1)
            inverse_std(NG - 1, 1)

        @block.scalar
        def _(act):
            for dst, src in ((row_add_sb, row_add), (pos_sb, pos_rows)):
                act.dma_start(dst[:], src).then_inc(embed_loaded, 16)
            for dst, src in ((ident32_sb, ident32), (b_qkv_sb, b_qkv), (b_out_sb, b_out), (head_sel_sb, head_sel),
                             (prob_t.rearrange("p a i k -> p (a i k)"), causal)):
                act.dma_start(dst[:], src).then_inc(attn_loaded, 16)

            def copy_halves(n):
                for c in range(2):
                    act.wait_ge(xn_turned[0], 2 * n + c + 1)
                    act.activation(xn_t[:, 0, c, :], work_ps[1 + c][0:HD, 0:GW], ACT.Copy).then_inc(xt_high[0], 1)

            def copy_q(n):
                for c in range(2):
                    act.wait_ge(q_done, 2 * n + c + 1)
                    act.activation(q_t[:, c, :], work_ps[1 + c][0:HD, 0:GW], ACT.Identity, bias=b_qkv_sb[:, c:c + 1],
                                   scale=1.0 / SPLIT).then_inc(q_copied, 1)

            def copy_k(n):
                for c in range(2):
                    act.wait_ge(k_done, 2 * n + c + 1)
                    act.activation(k_t[:, c, :], work_ps[c][0:HD, 0:GT], ACT.Identity, bias=b_qkv_sb[:, 2 + c:3 + c],
                                   scale=1.0 / SPLIT).then_inc(k_copied, 1)

            def copy_v(n, pairs):
                for j in pairs:
                    act.wait_ge(v_done, PAIRS * n + j + 1)
                    if not is_first(n):
                        act.wait_ge(att_done, PAIRS * (n - 1) + j + 1)
                    src = work_ps[V_BANK[j]][0:TOK, 0:DIM].rearrange("p (a b d) -> p a b d", b=2, d=HDIM)
                    for b in range(2):
                        act.activation(v_bd[SLOT * b:SLOT * b + TOK, 2 * j, :, b, :], src[:, :, b, :], ACT.Copy,
                                       scale=1.0 / SPLIT).then_inc(v_act, 1)

            def exps(g, p):
                act.wait_ge(shift_done, PAIRS * g + p + 1)
                act.activation(prob[p][:, :, 0:TOK], prob[p][:, :, 0:TOK], ACT.Exp).then_inc(exp_done, 1)

            def copy_prob(g, p):
                for s in range(2):
                    act.wait_ge(prob_turned, 2 * (PAIRS * g + p) + s + 1)
                    src = turn_ps[s][:, 0:384].rearrange("p (a i t) -> p a i t", a=3, i=2)[:, :, :, 0:TOK]
                    act.activation(prob_t[:, 3 * s:3 * s + 3, :, :], src, ACT.Copy).then_inc(prob_copied, 1)

            def copy_att(g):
                act.wait_ge(att_done, PAIRS * g + PAIRS)
                for c in range(2):
                    act.activation(att_t[:, c, 0:GT], att_ps[c][0:HD, 0:GT], ACT.Identity,
                                   bias=b_qkv_sb[:, 4 + c:5 + c]).then_inc(att_copied, 1)

            def copy_high2(n):
                for c in range(2):
                    act.wait_ge(xn_turned[1], 2 * n + c + 1)
                    act.activation(xs[:, c, at(n * GT, GT)], work_ps[2 - c][0:HD, 0:GT], ACT.Copy).then_inc(xt_high[1], 1)

            def split_high(g):
                if is_first(g):
                    act.wait_ge(expert_loaded, 16 * EXPERT_LOADS)
                for w, n in ((w1_sb, SLICE1), (w2_sb, SLICE2)):
                    act.activation(w[:, at(g * n, n)], w[:, at(g * n, n)], ACT.Copy, scale=SPLIT).then_inc(w_scaled, 1)
                act.wait_ge(w_scaled, g * 2 + 2)
                for hl, w, n in ((w1_hl, w1_sb, SLICE1), (w2_hl, w2_sb, SLICE2)):
                    act.activation(hl[:, 0, at(g * n, n)], w[:, at(g * n, n)], ACT.Copy).then_inc(w_high, 1)

            def group(g):
                if not is_first(g):
                    copy_prob(g - 1, 2)
                    copy_prob(g - 1, 3)
                exps(g, 0)
                copy_v(g, range(3))
                if not is_first(g):
                    copy_att(g - 1)
                copy_v(g, (3,))
                copy_prob(g, 0)
                exps(g, 1)
                if not is_last(g):
                    copy_halves(g + 1)
                copy_prob(g, 1)
                exps(g, 2)
                split_high(g)
                if not is_last(g):
                    copy_q(g + 1)
                if not is_last(g):
                    copy_k(g + 1)
                exps(g, 3)
                if not is_first(g):
                    copy_high2(g - 1)

            act.wait_ge(qkv_full, 4)
            act.activation(qkv_hl[:, 0, :, :], w_in_sb[:], ACT.Copy, scale=SPLIT).then_inc(qkv_high, 1)
            copy_halves(0)
            copy_q(0)
            copy_k(0)
            act.wait_ge(zeroed, 11)
            group(0)
            group(1)
            with act.Fori(2, NG - 2) as g:
                group(g)
            group(NG - 2)
            group(NG - 1)
            copy_prob(NG - 1, 2)
            copy_prob(NG - 1, 3)
            copy_att(NG - 1)
            copy_high2(NG - 1)

            act.wait_ge(routing, 3)
            act.activation(score_e[:], logit_s[:], ACT.Exp).then_inc(scores_exp, 1)

            act.wait_ge(places_ready, 2)
            act.wait_ge(xt_low[1], 2 * NG)
            place_regs = [act.alloc_register(f"act_place{i}") for i in range(4)]
            with act.Fori(0, IMAGES // 8) as b:
                for k, to in enumerate(places(act, place_regs, b * 8 + 4)):
                    act.activation(x_sorted[:, :, at(to, TOK)], xs[:, :, at((b * 8 + (4 + k)) * TOK, TOK)], ACT.Copy)\
                        .then_inc(sorted_act, 1)

            def gelu(j, e, first):
                for m in range(FM):
                    act.wait_ge(hid_done, j * FM + m + 1)
                    if not (first and m < 2):
                        act.wait_ge(hid_low, j * FM + (m - 1))
                    act.activation(hid[m % 2][:], gelu_ps[m][:, 0:BW], ACT.Gelu, bias=b1_sb[:, at(e * FM + m, 1)],
                                   scale=1.0 / SPLIT).then_inc(gelu_done, 1)

            def copy_y(j, e):
                for c in range(2):
                    act.wait_ge(y_done, j * 2 + c + 1)
                    act.activation(y_sorted[:, c, at(j * BW, BW)], y_ps[c][0:HD, 0:BW], ACT.Identity,
                                   bias=b2_sb[:, at(e * 2 + c, 1)], scale=1.0 / SPLIT).then_inc(y_copied, 1)

            def expert_of(j):
                return act.value_load(expert_i[0:1, at(j, 1)], min_val=0, max_val=EXPERTS - 1)

            gelu(0, expert_of(0), True)
            with act.Fori(1, BLOCKS) as j:
                gelu(j, expert_of(j), False)
                copy_y(j - 1, expert_of(j - 1))
            copy_y(BLOCKS - 1, expert_of(BLOCKS - 1))

            for c in range(2):
                act.wait_ge(y_copied, 2 * BLOCKS)
            place_regs += [act.alloc_register(f"act_place{i}") for i in range(4, GI)]
            for t in range(NG * TILES):
                if t % TILES == 0:
                    of = places(act, place_regs, t // TILES * GI)
                if t >= 3:
                    act.wait_ge(y_turned, t - 2)
                for k in range(2):
                    act.activation(y_tile[t % 3][:, :, k * TOK:(k + 1) * TOK],
                                   y_sorted[:, :, at(of[t % TILES * TI + k], TOK)], ACT.Copy).then_inc(picked_act, 1)

        @block.tensor
        def _(pe):
            def wait_for(*counts):
                for signal, count in counts:
                    pe.wait_ge(signal, count)

            def embed(n, part, *free):
                patches = x_sb
                if isinstance(n, int) and n == 1:
                    patches = x1_sb
                    pe.wait_ge(x1_loaded, 16)
                elif is_first(n):
                    pe.wait_ge(x_loaded, 16)
                else:
                    pe.wait_ge(x_loaded, n * 16)
                wait_for(*free)
                for i, t in enumerate(((0, 1), (2,))[part]):
                    for k in range(PK):
                        mm = pe.matmul(work_ps[0][0:TT, i * DIM:(i + 1) * DIM], patches[:, k, t * TT:(t + 1) * TT],
                                       tok_w_sb[:, k, :], start=(k == 0), stop=(k == PK - 1))
                mm.then_inc(embedded, 1)

            def turn(n, w, banks, *free):
                pe.wait_ge(xn_ready[w], n * TILES + TILES)
                for c in range(2):
                    wait_for(*free[c])
                    for t in range(TILES):
                        mm = pe.transpose(work_ps[banks[c]][0:HD, t * TT:(t + 1) * TT],
                                          xn[w][:, t, c * HD:(c + 1) * HD], ident32_sb[0:TT, 0:TT])
                    mm.then_inc(xn_turned[w], 1)

            def queries_keys(n, *free):
                pe.wait_ge(xt_low[0], n * 2 + 2)
                pe.wait_ge(xt_high[0], n * 2 + 2)
                for o, c, cols, bank, done in ((0, 0, GW, 1, q_done), (0, 1, GW, 2, q_done),
                                               (DIM, 0, GT, 0, k_done), (DIM, 1, GT, 1, k_done)):
                    if done is k_done and c == 0:
                        wait_for(*free)
                    if done is k_done and c == 1:
                        pe.wait_ge(q_copied, n * 2 + 1)
                    i = 0
                    for kc in range(2):
                        for wh, xh in ((0, 0), (0, 1), (1, 0)):
                            mm = pe.matmul(work_ps[bank][0:HD, 0:cols],
                                           qkv_hl[:, wh, kc, o + c * HD:o + (c + 1) * HD],
                                           xn_t[:, xh, kc, 0:cols], start=(i == 0), stop=(i == 5))
                            i += 1
                    mm.then_inc(done, 1)

            def values(n, pairs, *free):
                for j in pairs:
                    wait_for(*(free[j] if j < 3 else pair_out(n, 0)))
                    for b in range(2):
                        t0 = (2 * j + b) * TOK
                        i = 0
                        for kc in range(2):
                            for wh, xh in ((0, 0), (0, 1), (1, 0)):
                                mm = pe.matmul(work_ps[V_BANK[j]][SLOT * b:SLOT * b + SLOT, 0:DIM],
                                               xn_t[:, xh, kc, t0:t0 + SLOT], qkv_hl[:, wh, kc, 2 * DIM:3 * DIM],
                                               start=(i == 0), stop=(i == 5))
                                i += 1
                    mm.then_inc(v_done, 1)

            def scores(g, p):
                if p == 0:
                    for s in (k_spread_dve, k_spread_pool, q_copied):
                        pe.wait_ge(s, g * 2 + 2)
                if not (is_first(g) and p == 0):
                    pe.wait_ge(shift_done, g * PAIRS + p)
                s = score_ps
                pe.matmul(s[:, 0:HEADS * TOK], ident16_sb[:], causal_sb[:], start=True, stop=True)
                for i in range(2):
                    im = 2 * p + i
                    for c in range(2):
                        mm = pe.matmul(s[SLOT * i:SLOT * i + SLOT, c * HP * TOK:(c + 1) * HP * TOK],
                                       q_t[:, c, im * TOK:im * TOK + SLOT], k_x[:, c, im, :, :],
                                       start=False, stop=True, skip_group_check=True)
                mm.then_inc(scored, 1)

            def turn_prob(g, p):
                pe.wait_ge(prob_ready, g * PAIRS + p + 1)
                for s in range(2):
                    if not (is_first(g) and p == 0):
                        pe.wait_ge(prob_copied, (g * PAIRS + p - 1) * 2 + s + 1)
                    for a in range(3):
                        i = 3 * s + a
                        mm = pe.transpose(turn_ps[s][:, a * 128:(a + 1) * 128], prob[p][:, 2 * i:2 * i + 2, :],
                                          ident32_sb[:])
                    mm.then_inc(prob_turned, 1)

            def weigh(g, p):
                pe.wait_ge(prob_copied, (g * PAIRS + p) * 2 + 2)
                if p == 0:
                    pe.wait_ge(v_act, g * 2 * PAIRS + 2 * PAIRS)
                    pe.wait_ge(v_dve, g * 2 * PAIRS + 2 * PAIRS)
                    if not is_first(g):
                        pe.wait_ge(att_copied, g * 2)
                for i in range(2):
                    im = 2 * p + i
                    for a in range(HP):
                        r = 32 * (a % 3)
                        mm = pe.matmul(att_ps[a // 3][r:r + 32, im * TOK:(im + 1) * TOK],
                                       v_bd[:, im, a, :, :], prob_t[:, a, i, :], start=True, stop=True)
                mm.then_inc(att_done, 1)

            def project(n, *free):
                pe.wait_ge(att_copied, n * 2 + 2)
                for part, (bank, tiles) in enumerate(((2, (0, 1)), (0, (2,)))):
                    wait_for(*free[part])
                    for i, t in enumerate(tiles):
                        for c in range(2):
                            mm = pe.matmul(work_ps[bank][0:TT, i * DIM:(i + 1) * DIM],
                                           att_t[:, c, t * TT:(t + 1) * TT], w_out_sb[:, c, :],
                                           start=(c == 0), stop=(c == 1))
                    mm.then_inc(projected, 1)

            def pair_out(n, j):
                return (v_act, n * 2 * PAIRS + 2 * j + 2), (v_dve, n * 2 * PAIRS + 2 * j + 2)

            def turned_out(n, w, c):
                sums = ((token_sum, n * 2 + c + 1),) if w else ()
                return (xt_high[w], n * 2 + c + 1), (xt_low[w], n * 2 + c + 1), *sums

            def group(g):
                if not is_first(g):
                    turn_prob(g - 1, 2)
                if not is_late(g):
                    embed(g + 2, 0, (k_copied, g * 2 + 1))
                if not is_first(g):
                    weigh(g - 1, 2)
                scores(g, 0)
                if not is_first(g):
                    turn_prob(g - 1, 3)
                third = (k_copied, g * 2 + 1) if is_late(g) else (h_ready, g * 2 + 5)
                if isinstance(g, int) and g < 2:
                    values(g, range(3), ((k_copied, g * 2 + 2),), ((q_copied, g * 2 + 2),), (third,))
                else:
                    values(g, range(3), turned_out(g - 2, 1, 1), turned_out(g - 2, 1, 0), (third,))
                if not is_first(g):
                    weigh(g - 1, 3)
                scores(g, 1)
                values(g, (3,))
                turn_prob(g, 0)
                if not is_first(g):
                    project(g - 1, pair_out(g, 1), pair_out(g, 2))
                weigh(g, 0)
                if not is_last(g):
                    turn(g + 1, 0, (1, 2), pair_out(g, 3),
                         pair_out(g, 1) if is_first(g) else ((h2_ready, g * 2 - 1),))
                scores(g, 2)
                turn_prob(g, 1)
                if not is_late(g):
                    embed(g + 2, 1, *(pair_out(g, 2) if is_first(g) else ((h2_ready, g * 2),)))
                weigh(g, 1)
                scores(g, 3)
                if not is_last(g):
                    queries_keys(g + 1, (h2_ready, g * 2) if is_late(g) else (h_ready, g * 2 + 6))
                if is_last(g):
                    turn(g - 1, 1, (2, 1), ((h2_ready, g * 2 - 1),), pair_out(g, 3))
                elif not is_first(g):
                    turn(g - 1, 1, (2, 1), ((q_copied, g * 2 + 4),), ((k_copied, g * 2 + 4),))

            pe.wait_ge(zeroed, 11)
            pe.wait_ge(embed_loaded, 16 * 3)
            embed(0, 0)
            pe.wait_ge(lora_loaded, 16 * 4)
            for kc in range(2):
                for s in range(2):
                    pe.matmul(lora_ps[2 * kc + s][0:HD, 0:288], lora_in_sb[:, kc * HD:(kc + 1) * HD],
                              lora_in_sb[:, DIM + s * 288:DIM + (s + 1) * 288], start=True, stop=True)\
                        .then_inc(lora_done, 1)
            for kc in range(2):
                pe.matmul(turn_ps[kc][0:HD, 0:DIM], lora_out_sb[:, kc * HD:(kc + 1) * HD],
                          lora_out_sb[:, DIM:2 * DIM], start=True, stop=True).then_inc(lora_done, 1)
            embed(0, 1, (h_ready, 1))
            embed(1, 0, (h_ready, 2))
            pe.wait_ge(attn_loaded, 16 * ATTN_LOADS)
            turn(0, 0, (1, 2), ((qkv_full, 4),), ((qkv_full, 4),))
            embed(1, 1, (h_ready, 3))
            pe.wait_ge(qkv_high, 1)
            pe.wait_ge(qkv_low, 1)
            queries_keys(0, (h_ready, 4))
            pe.wait_ge(out_full, 2)
            pe.wait_ge(mask_ready, 2)
            group(0)
            group(1)
            with pe.Fori(2, NG - 2) as g:
                group(g)
            group(NG - 2)
            group(NG - 1)
            turn_prob(NG - 1, 2)
            weigh(NG - 1, 2)
            turn_prob(NG - 1, 3)
            weigh(NG - 1, 3)
            project(NG - 1, turned_out(NG - 2, 1, 0), ((h2_ready, NG * 2 - 2),))
            turn(NG - 1, 1, (2, 1), ((h2_ready, NG * 2 - 1),), turned_out(NG - 2, 1, 1))

            pe.wait_ge(token_sum, 2 * NG)
            pe.wait_ge(expert_loaded, 16 * EXPERT_LOADS)
            for c in range(2):
                mm = pe.matmul(score_ps[0:IMAGES, 0:EXPERTS], x_sum[:, c, :], wg_sb[:, c, :],
                               start=(c == 0), stop=(c == 1))
            mm.then_inc(logits_done, 1)
            pe.wait_ge(routing, 8)
            pe.wait_ge(expert_loaded, 16 * EXPERT_LOADS)
            pe.matmul(att_ps[0][0:IMAGES, 0:EXPERTS], order_sb[:, 0:IMAGES], chosen[:], start=True, stop=True)
            pe.matmul(att_ps[0][0:IMAGES, EXPERTS:2 * EXPERTS], order_sb[:, IMAGES:2 * IMAGES], chosen[:],
                      start=True, stop=True).then_inc(ranked, 1)
            pe.wait_ge(placed, 1)
            pe.matmul(turn_ps[0][0:1, 0:IMAGES], place[:], ident32_sb[0:IMAGES, 0:IMAGES], start=True, stop=True)\
                .then_inc(gates_spread, 1)
            pe.matmul(turn_ps[1][0:TT, 0:NG * TILES], slot_sel_sb[:], gate_tile[:], start=True, stop=True)\
                .then_inc(gates_spread, 1)

            def expert_of(j):
                return pe.value_load(expert_i[0:1, at(j, 1)], min_val=0, max_val=EXPERTS - 1)

            def hidden(j, e, m, first):
                if not first:
                    pe.wait_ge(gelu_done, j * FM + (m + 1 - FM))
                i = 0
                for kc in range(2):
                    for wh, xh in ((0, 0), (0, 1), (1, 0)):
                        mm = pe.matmul(gelu_ps[m][:, 0:BW],
                                       w1_hl[:, wh, at(e * (2 * FFN) + (kc * FFN + m * 128), 128)],
                                       x_sorted[:, 2 * xh + kc, at(j * BW, BW)], start=(i == 0), stop=(i == 5))
                        i += 1
                mm.then_inc(hid_done, 1)

            def outputs(j, e, par, m, first):
                pe.wait_ge(hid_high, j * FM + (m + 1))
                pe.wait_ge(hid_low, j * FM + (m + 1))
                for c in range(2):
                    if m == 0 and not first:
                        pe.wait_ge(y_copied, j * 2 + c - 1)
                    for i, (wh, xh) in enumerate(((0, 0), (0, 1), (1, 0))):
                        mm = pe.matmul(y_ps[c][0:HD, 0:BW],
                                       w2_hl[:, wh, at(e * (FM * DIM) + (m * DIM + c * HD), HD)],
                                       hid_hl[:, par, xh, m, :] if isinstance(par, int) else
                                       hid_hl[:, at(par, 1), xh, m, :].rearrange("p a t -> p (a t)"),
                                       start=(m == 0 and i == 0), stop=(m == FM - 1 and i == 2),
                                       skip_group_check=True)
                    if m == FM - 1:
                        mm.then_inc(y_done, 1)

            pe.wait_ge(places_ready, 2)
            pe.wait_ge(gates_ready, 1)
            pe.wait_ge(sorted_dve, IMAGES // 2)
            pe.wait_ge(sorted_act, IMAGES // 2)
            pe.wait_ge(w_low, 2 * NG)
            pe.wait_ge(w_high, 2 * NG)
            e = expert_of(0)
            for m in range(FM):
                hidden(0, e, m, True)
            e1, e0 = expert_of(1), expert_of(0)
            for m in range(FM):
                hidden(1, e1, m, False)
                outputs(0, e0, 0, m, True)
            with pe.Fori(2, BLOCKS) as j:
                e1, e0 = expert_of(j), expert_of(j - 1)
                par = pe.snap((j - 1) & 1)
                for m in range(FM):
                    hidden(j, e1, m, False)
                    outputs(j - 1, e0, par, m, False)
            e0 = expert_of(BLOCKS - 1)
            for m in range(FM):
                outputs(BLOCKS - 1, e0, (BLOCKS - 1) % 2, m, False)

            for t in range(NG * TILES):
                pe.wait_ge(picked_act, 2 * t + 2)
                pe.wait_ge(picked_dve, t + 1)
                if t >= 3:
                    pe.wait_ge(out_ready, t - 2)
                for c in range(2):
                    mm = pe.transpose(work_ps[t % 3][0:TT, c * HD:(c + 1) * HD], y_tile[t % 3][:, c, :],
                                      ident32_sb[0:HD, 0:HD])
                mm.then_inc(y_turned, 1)

        @block.vector
        def _(dve):
            def add_positions(n, part):
                a, b = ((0, 2), (2, 1))[part]
                dve.wait_ge(embedded, n * 2 + part + 1)
                dve.tensor_tensor(h[:, at(n * TILES + a, b), :],
                                  work_ps[0][0:TT, 0:b * DIM].rearrange("p (a d) -> p a d", d=DIM),
                                  pos_sb[:].unsqueeze(1).broadcast_to([TT, b, DIM]), ALU.add).then_inc(h_ready, 1)

            def add_attention(n):
                dve.wait_ge(bias_added, n + 1)
                for part, (a, b) in enumerate(((0, 2), (2, 1))):
                    dve.wait_ge(projected, n * 2 + part + 1)
                    dve.tensor_tensor(h[:, at(n * TILES + a, b), :],
                                      work_ps[2 - 2 * part][0:TT, 0:b * DIM].rearrange("p (a d) -> p a d", d=DIM),
                                      h[:, at(n * TILES + a, b), :], ALU.add).then_inc(h2_ready, 1)

            def moments(n, w):
                dve.wait_ge(attn_loaded, 16 * ATTN_LOADS)
                dve.wait_ge((h_ready, h2_ready)[w], n * 2 + 2)
                for t in range(TILES):
                    dve.bn_stats(stats[w][:, t, :], h[:, at(n * TILES + t, 1), :].rearrange("p a d -> p (a d)"))\
                        .then_inc(stats_done[w], 1)
                dve.wait_ge(stats_done[w], n * TILES + TILES)

            def aggregate(w):
                for t in range(TILES):
                    dve.bn_aggr(mean_var[w][:, t, :], stats[w][:, t, :]).then_inc(aggr_done[w], 1)

            def norm(n, w):
                dve.wait_ge(rstd_done[w], n + 1)
                if not is_first(n):
                    dve.wait_ge(xn_turned[w], n * 2)
                for t in range(TILES):
                    dve.tensor_scalar(xn[w][:, t, :], h[:, at(n * TILES + t, 1), :].rearrange("p a d -> p (a d)"),
                                      mean_var[w][:, t, 0:1], rstd[w][:, t:t + 1], ALU.subtract, ALU.mult)\
                        .then_inc(xn_ready[w], 1)

            def low_halves(n):
                for c in range(2):
                    dve.wait_ge(xt_high[0], n * 2 + c + 1)
                    dve.tensor_tensor(xn_t[:, 1, c, :], work_ps[1 + c][0:HD, 0:GW], xn_t[:, 0, c, :], ALU.subtract)\
                        .then_inc(xt_low[0], 1)

            def low_halves2(n):
                for c in range(2):
                    dve.wait_ge(xt_high[1], n * 2 + c + 1)
                    dve.tensor_tensor(xs[:, 2 + c, at(n * GT, GT)], work_ps[2 - c][0:HD, 0:GT], xs[:, c, at(n * GT, GT)],
                                      ALU.subtract).then_inc(xt_low[1], 1)
                    dve.tensor_reduce(x_sum[:, c, at(n * GI, GI)],
                                      work_ps[2 - c][0:HD, 0:GT].rearrange("p (i k) -> p i k", k=TOK), AX, ALU.add)\
                        .then_inc(token_sum, 1)

            def spread_keys(n):
                for c in range(2):
                    dve.wait_ge(k_copied, n * 2 + c + 1)
                    spread(dve, c, 0, POOL_HEADS).then_inc(k_spread_dve, 1)

            def copy_v(n, pairs):
                for j in pairs:
                    dve.wait_ge(v_act, n * 2 * PAIRS + 2 * j + 2)
                    if not is_first(n):
                        dve.wait_ge(att_done, PAIRS * (n - 1) + j + 1)
                    src = work_ps[V_BANK[j]][SLOT:SLOT + TOK, 0:DIM].rearrange("p (a b d) -> p a b d", b=2, d=HDIM)
                    for b in range(2):
                        dve.tensor_scalar(v_bd[SLOT * b:SLOT * b + TOK, 2 * j + 1, :, b, :], src[:, :, b, :],
                                          1.0 / SPLIT, None, ALU.mult).then_inc(v_dve, 1)

            def shift(g, p):
                s = score_ps[:, 0:HEADS * TOK].rearrange("p (a k) -> p a k", k=TOK)
                dve.wait_ge(scored, g * PAIRS + p + 1)
                dve.tensor_reduce(row_max[p % 2][:], s, AX, ALU.max).then_inc(max_done, 1)
                dve.wait_ge(max_done, g * PAIRS + p + 1)
                if not is_first(g):
                    dve.wait_ge(prob_turned, 2 * PAIRS * (g - 1) + 2 * p + 2)
                dve.tensor_tensor(prob[p][:, :, 0:TOK], s,
                                  row_max[p % 2][:].unsqueeze(2).broadcast_to([128, HEADS, TOK]), ALU.subtract)\
                    .then_inc(shift_done, 1)

            def sums(g, p):
                dve.wait_ge(exp_done, g * PAIRS + p + 1)
                dve.tensor_reduce(row_sum[p % 2][:], prob[p][:, :, 0:TOK], AX, ALU.add).then_inc(sum_done, 1)
                dve.wait_ge(sum_done, g * PAIRS + p + 1)
                if not (is_first(g) and p < 2):
                    dve.wait_ge(prob_ready, g * PAIRS + (p - 1))
                dve.reciprocal(inv_sum[p % 2][:], row_sum[p % 2][:]).then_inc(inv_done, 1)

            def group(g):
                if not is_late(g):
                    add_positions(g + 2, 0)
                shift(g, 0)
                sums(g, 0)
                copy_v(g, range(3))
                shift(g, 1)
                copy_v(g, (3,))
                sums(g, 1)
                if not is_first(g):
                    add_attention(g - 1)
                    moments(g - 1, 1)
                if not is_last(g):
                    low_halves(g + 1)
                if not is_first(g):
                    aggregate(1)
                shift(g, 2)
                if not is_late(g):
                    add_positions(g + 2, 1)
                    moments(g + 2, 0)
                if not is_first(g):
                    norm(g - 1, 1)
                sums(g, 2)
                if not is_late(g):
                    aggregate(0)
                shift(g, 3)
                if not is_late(g):
                    norm(g + 2, 0)
                if not is_last(g):
                    spread_keys(g + 1)
                sums(g, 3)
                if not is_first(g):
                    low_halves2(g - 1)

            dve.memset(sort_room[0:HD, PK * GW:], 0.0).then_inc(zeroed, 1)
            dve.wait_ge(pos_added, 1)
            add_positions(0, 0)
            dve.wait_ge(lora_loaded, 16 * 4)
            for kc in range(2):
                for s in range(2):
                    dve.wait_ge(lora_done, 2 * kc + s + 1)
                    w = w_in_sb[:, kc, s * 288:(s + 1) * 288]
                    dve.scalar_tensor_tensor(out=w, in0=lora_ps[2 * kc + s][0:HD, 0:288], scalar=LORA, in1=w,
                                             op0=ALU.mult, op1=ALU.add).then_inc(qkv_full, 1)
            add_positions(0, 1)
            moments(0, 0)
            aggregate(0)
            dve.wait_ge(qkv_high, 1)
            dve.scalar_tensor_tensor(out=qkv_hl[:, 1, :, :], in0=w_in_sb[:], scalar=SPLIT, in1=qkv_hl[:, 0, :, :],
                                     op0=ALU.mult, op1=ALU.subtract).then_inc(qkv_low, 1)
            norm(0, 0)
            add_positions(1, 0)
            low_halves(0)
            add_positions(1, 1)
            moments(1, 0)
            aggregate(0)
            dve.wait_ge(lora_done, 6)
            for kc in range(2):
                w = w_out_sb[:, kc, :]
                dve.scalar_tensor_tensor(out=w, in0=turn_ps[kc][0:HD, 0:DIM], scalar=LORA, in1=w,
                                         op0=ALU.mult, op1=ALU.add).then_inc(out_full, 1)
            spread_keys(0)
            norm(1, 0)
            dve.wait_ge(zeroed, 11)
            group(0)
            group(1)
            with dve.Fori(2, NG - 2) as g:
                group(g)
            group(NG - 2)
            group(NG - 1)
            add_attention(NG - 1)
            moments(NG - 1, 1)
            aggregate(1)
            norm(NG - 1, 1)
            low_halves2(NG - 1)

            step = 0

            def then(ins):
                nonlocal step
                step += 1
                ins.then_inc(routing, 1)
                dve.wait_ge(routing, step)

            dve.wait_ge(logits_done, 1)
            then(dve.tensor_scalar(logit[:], score_ps[0:IMAGES, 0:EXPERTS], 1.0 / TOK, None, ALU.mult))
            then(dve.tensor_reduce(top[:], logit[:], AX, ALU.max))
            then(dve.tensor_scalar(logit_s[:], logit[:], top[:], None, ALU.subtract))
            then(dve.tensor_scalar(is_top[:], logit[:], top[:], None, ALU.is_equal))
            then(dve.tensor_scalar(not_first[:], is_top[:, 0:1], -1.0, 1.0, ALU.mult, ALU.add))
            then(dve.tensor_copy(chosen[:, 0:1], is_top[:, 0:1]))
            then(dve.tensor_tensor(chosen[:, 1:2], is_top[:, 1:2], not_first[:], ALU.mult))
            then(dve.tensor_tensor(chosen[:, 2:3], not_first[:], chosen[:, 1:2], ALU.subtract))
            dve.wait_ge(scores_exp, 1)
            then(dve.tensor_reduce(score_s[:], score_e[:], AX, ALU.add))
            then(dve.reciprocal(gate[:], score_s[:]))
            dve.wait_ge(expert_loaded, 16 * EXPERT_LOADS)
            then(dve.tensor_scalar(gate_tile[:], tile_sel_sb[:], gate[:], None, ALU.mult))
            dve.wait_ge(ranked, 1)
            then(dve.tensor_tensor(over[:],
                                   att_ps[0][0:IMAGES, EXPERTS:2 * EXPERTS].unsqueeze(2)
                                   .broadcast_to([IMAGES, EXPERTS, ROUND]),
                                   steps_sb[:, 0:ROUND].unsqueeze(1).broadcast_to([IMAGES, EXPERTS, ROUND]),
                                   ALU.is_gt))
            then(dve.tensor_reduce(n_block[:], over[:], AX, ALU.add))
            then(dve.memset(start[:, 0:1], 0.0))
            then(dve.tensor_copy(start[:, 1:2], n_block[:, 0:1]))
            then(dve.tensor_tensor(start[:, 2:3], n_block[:, 0:1], n_block[:, 1:2], ALU.add))
            then(dve.scalar_tensor_tensor(out=place_e[:], in0=start[:], scalar=float(BI),
                                          in1=att_ps[0][0:IMAGES, 0:EXPERTS], op0=ALU.mult, op1=ALU.add))
            then(dve.scalar_tensor_tensor(out=place_c[:], in0=place_e[:], scalar=float(TOK), in1=chosen[:],
                                          op0=ALU.mult, op1=ALU.mult))
            dve.tensor_reduce(place[:], place_c[:], AX, ALU.add).then_inc(placed, 1)
            for k in range(2):
                then(dve.tensor_scalar(begun[:, k, :], steps_sb[0:1, ROUND:], start[0:1, k + 1:k + 2], None,
                                       ALU.is_ge))
            dve.tensor_tensor(expert_i[:], begun[:, 0, :], begun[:, 1, :], ALU.add).then_inc(places_ready, 1)
            dve.wait_ge(gates_spread, 1)
            dve.tensor_copy(place_i[:], turn_ps[0][0:1, 0:IMAGES]).then_inc(places_ready, 1)
            dve.wait_ge(gates_spread, 2)
            dve.tensor_copy(gate_tok[:], turn_ps[1][0:TT, 0:NG * TILES]).then_inc(gates_ready, 1)

            dve.wait_ge(places_ready, 2)
            dve.wait_ge(zeroed, 12)
            dve.wait_ge(xt_high[1], 2 * NG)
            dve.wait_ge(xt_low[1], 2 * NG)
            place_regs = [dve.alloc_register(f"dve_place{i}") for i in range(4)]
            with dve.Fori(0, IMAGES // 8) as b:
                for k, to in enumerate(places(dve, place_regs, b * 8)):
                    dve.tensor_copy(x_sorted[:, :, at(to, TOK)], xs[:, :, at((b * 8 + k) * TOK, TOK)])\
                        .then_inc(sorted_dve, 1)

            def halves(j, par, first):
                if not first:
                    dve.wait_ge(y_done, j * 2 - 2)
                for m in range(FM):
                    hh, hl = (hid_hl[:, par, k, m, :] if isinstance(par, int) else
                              hid_hl[:, at(par, 1), k, m, :].rearrange("p a t -> p (a t)") for k in range(2))
                    dve.wait_ge(gelu_done, j * FM + (m + 1))
                    dve.tensor_copy(hh, hid[m % 2][:]).then_inc(hid_high, 1)
                    dve.wait_ge(hid_high, j * FM + (m + 1))
                    dve.tensor_tensor(hl, hid[m % 2][:], hh, ALU.subtract).then_inc(hid_low, 1)

            halves(0, 0, True)
            halves(1, 1, True)
            with dve.Fori(2, BLOCKS) as j:
                par = dve.snap(j & 1)
                halves(j, par, False)

            place_regs += [dve.alloc_register(f"dve_place{i}") for i in range(4, GI)]

            def pick(t, of):
                if t >= 3:
                    dve.wait_ge(y_turned, t - 2)
                k = TI - 1
                at_k = of[min(t % TILES * TI + k, GI - 1)]
                dve.tensor_copy(y_tile[t % 3][:, :, k * TOK:(k + 1) * TOK], y_sorted[:, :, at(at_k, TOK)])\
                    .then_inc(picked_dve, 1)

            dve.wait_ge(y_copied, 2 * BLOCKS)
            for t in range(NG * TILES + 1):
                if t < NG * TILES:
                    if t % TILES == 0:
                        of = places(dve, place_regs, t // TILES * GI)
                    pick(t, of)
                if t >= 1:
                    dve.wait_ge(y_turned, t)
                    if t > OUTS:
                        dve.wait_ge(stored[(t - 1) % OUTS], 16 * ((t - 1) // OUTS))
                    dve.scalar_tensor_tensor(out=out_sb[(t - 1) % OUTS], in0=work_ps[(t - 1) % 3][0:TT, 0:DIM],
                                             scalar=gate_tok[:, t - 1:t], in1=h[:, t - 1, :],
                                             op0=ALU.mult, op1=ALU.add).then_inc(out_ready, 1)


def _laid_out(x, L0_tok_W, L0_tok_b, L0_tok_cls_token, L0_tok_pos_table, L0_attn_w_in, L0_attn_b_in, L0_attn_A_in,
              L0_attn_B_in, L0_attn_w_out, L0_attn_b_out, L0_attn_A_out, L0_attn_B_out, L0_ffn_Wg, L0_ffn_W1,
              L0_ffn_b1, L0_ffn_W2, L0_ffn_b2):
    a = {k: np.asarray(v) for k, v in locals().items()}
    f = np.float32
    p = a["x"].reshape(IMAGES, GRID, PATCH, GRID, PATCH, 3).transpose(0, 1, 3, 2, 4, 5)
    p = p.reshape(IMAGES, TOK - 1, PIX)
    p = np.concatenate([np.zeros((IMAGES, 1, PIX), f), p], axis=1)
    cls = a["L0_tok_cls_token"].reshape(1, DIM)
    rows = np.concatenate([cls, np.broadcast_to(a["L0_tok_b"], (TOK - 1, DIM))], axis=0)
    b_in = a["L0_attn_b_in"].reshape(6, HD)
    image = np.arange(IMAGES)
    part = np.arange(HD)
    head_sel = (part[:, None] // HDIM == np.arange(HP)[None, :]).astype(f)
    q = np.arange(128)[:, None]
    k = np.tile(np.arange(TOK), HEADS)[None, :]
    hidden = (q % SLOT < TOK) & (k > q % SLOT)
    tile = image // GI * TILES + image % GI // TI
    slot = image % GI % TI
    steps = np.concatenate([BI * np.arange(ROUND), np.arange(BLOCKS)]).astype(f)
    return {
        "x": p.reshape(NG, GT, PK, 128).transpose(0, 3, 2, 1),
        "tok_w": a["L0_tok_W"].reshape(PK, 128, DIM).transpose(1, 0, 2),
        "row_add": np.tile(rows, (TI, 1)),
        "pos_rows": np.tile(a["L0_tok_pos_table"], (TI, 1)),
        "w_in": a["L0_attn_w_in"].reshape(2, HD, 3 * DIM).transpose(1, 0, 2),
        "lora_in": np.concatenate([a["L0_attn_B_in"].T, a["L0_attn_A_in"]], axis=1),
        "w_out": a["L0_attn_w_out"].reshape(2, HD, DIM).transpose(1, 0, 2),
        "lora_out": np.concatenate([a["L0_attn_B_out"].T, a["L0_attn_A_out"]], axis=1),
        "b_qkv": b_in.T,
        "b_out": np.tile(a["L0_attn_b_out"][None, :], (TT, 1)),
        "head_sel": head_sel,
        "causal": np.where(hidden, -1e9, 0.0).astype(f),
        "ident32": np.eye(128, dtype=f),
        "wg": a["L0_ffn_Wg"].T.reshape(2, HD, EXPERTS).transpose(1, 0, 2),
        "w1": a["L0_ffn_W1"].reshape(EXPERTS, 2, HD, FFN).transpose(2, 0, 1, 3).reshape(HD, -1),
        "b1": a["L0_ffn_b1"].reshape(EXPERTS * FM, 128).T,
        "w2": a["L0_ffn_W2"].reshape(EXPERTS, FM, 128, DIM).transpose(2, 0, 1, 3).reshape(128, -1),
        "b2": a["L0_ffn_b2"].reshape(EXPERTS * 2, HD).T,
        "order": np.concatenate([np.triu(np.ones((IMAGES, IMAGES)), 1), np.ones((IMAGES, IMAGES))], 1).astype(f),
        "tile_sel": (tile[:, None] == np.arange(NG * TILES)[None, :]).astype(f),
        "slot_sel": (slot[:, None] == np.arange(TT)[None, :] // TOK).astype(f),
        "steps": np.tile(steps[None, :], (IMAGES, 1)),
    }


def kernel(**inputs):
    import concourse.bacc as bacc
    from concourse.bass_utils import run_bass_kernel_spmd

    arrays = {k: np.ascontiguousarray(v) for k, v in _laid_out(**inputs).items()}
    nc = bacc.Bacc("TRN2", target_bir_lowering=False, num_devices=1)
    aps = {k: nc.dram_tensor(f"in_{k}", v.shape, mybir.dt.from_np(v.dtype), kind="ExternalInput").ap()
           for k, v in arrays.items()}
    out = nc.dram_tensor("out", (IMAGES * TOK, DIM), F32, kind="ExternalOutput").ap()
    vit_layer(nc, **aps, out=out)
    r = run_bass_kernel_spmd(nc, [{f"in_{k}": v for k, v in arrays.items()}], core_ids=[0])
    return r.results[0]["out"].reshape(IMAGES, TOK, DIM)
```

```python
from contextlib import ExitStack

import numpy as np

import concourse.bass as bass
from concourse import mybir

F32 = mybir.dt.float32
F16 = mybir.dt.float16
BF16 = mybir.dt.bfloat16
I32 = mybir.dt.int32
ALU = mybir.AluOpType
ACT = mybir.ActivationFunctionType
AX = mybir.AxisListType.X

IMAGES = 64
PATCH = 16
GRID = 6
TOK = GRID * GRID + 1
PIX = PATCH * PATCH * 3
PK = PIX // 128
DIM = 192
REST = DIM - 128
HD = DIM // 2
HEADS = 12
HDIM = DIM // HEADS
HP = HEADS // 2
FFN = 768
FM = FFN // 128
EXPERTS = 3
LORA = 8.0
EPS = 1e-5
SPLIT = 64.0
PARTS = ((0, 0, 0), (0, 0, 1), (1, 0, 0), (0, 1, 2), (1, 1, 2))

GI = 8
NG = IMAGES // GI
GT = GI * TOK
TI = 3
TT = TI * TOK
TILES = -(-GI // TI)
GW = TILES * TT
PAIRS = GI // 2
SLOT = 64

BI = 9
BW = BI * TOK
BLOCKS = (IMAGES + EXPERTS * (BI - 1)) // BI
ROUND = 8


def vit_layer(nc, x, tok_w, row_add, pos_rows, w_in, lora_in, w_out, lora_out, b_qkv, b_out, head_sel, causal,
              ident32, wg, w1, b1, w2, b2, order, tile_sel, slot_sel, fold, steps, out):
    with ExitStack() as ctx:
        def sb(name, shape, dt=F32):
            return ctx.enter_context(nc.sbuf_tensor(name, shape, dt))

        def sem(name):
            return ctx.enter_context(nc.semaphore(name))

        at = bass.ds

        score_ps = ctx.enter_context(nc.psum_tensor("score_ps", [128, 512], F32))
        turn_ps = [ctx.enter_context(nc.psum_tensor(f"turn_ps{i}", [128, 512], F32)) for i in range(2)]
        att_ps = [ctx.enter_context(nc.psum_tensor(f"att_ps{i}", [128, 512], F32)) for i in range(2)]
        work_ps = [ctx.enter_context(nc.psum_tensor(f"work_ps{i}", [128, 512], F32)) for i in range(3)]

        gelu_ps = [score_ps, *turn_ps, *work_ps]
        y_ps = att_ps

        lora_ps = [work_ps[1], work_ps[2], score_ps, att_ps[0]]

        early = sb("early", [128, PK * GW + PK * DIM + 2 * 3 * DIM])
        x_sb = early[:, 0:PK * GW].rearrange("p (k t) -> p k t", k=PK)
        tok_w_sb = early[:, PK * GW:PK * (GW + DIM)].rearrange("p (k d) -> p k d", k=PK)
        row_add_sb = sb("row_add_sb", [TT, DIM])
        pos_sb = sb("pos_sb", [TT, DIM])
        w_in_sb = early[:, PK * (GW + DIM):].rearrange("p (k d) -> p k d", k=2)
        w_out_sb = sb("w_out_sb", [HD, 2, DIM])
        qkv_hl = sb("qkv_hl", [128, 2, 2, 3 * DIM], F16)
        b_qkv_sb = sb("b_qkv_sb", [HD, 6])
        b_out_sb = sb("b_out_sb", [TT, DIM])
        head_sel_sb = sb("head_sel_sb", [HD, HP])
        causal_sb = sb("causal_sb", [128, HEADS * TOK], BF16)
        ident16_sb = sb("ident16_sb", [128, 128], BF16)
        ident32_sb = sb("ident32_sb", [128, 128])
        wg_sb = sb("wg_sb", [128, 2, EXPERTS])
        staged = sb("staged", [128, EXPERTS * (2 * FFN + FM * DIM)])
        w1_sb = staged[:, 0:EXPERTS * 2 * FFN]
        w2_sb = staged[:, EXPERTS * 2 * FFN:]
        w1_hl = sb("w1_hl", [128, 2, EXPERTS * 2 * FFN], F16)
        w2a_hl = sb("w2a_hl", [128, 2, EXPERTS * FM * 128], F16)
        w2b_hl = sb("w2b_hl", [128, EXPERTS * FM * 2 * REST], F16)
        b1_sb = sb("b1_sb", [128, EXPERTS * FM])
        b2_sb = sb("b2_sb", [128, EXPERTS * 2])
        fold_sb = sb("fold_sb", [128, REST])
        order_sb = sb("order_sb", [IMAGES, 2 * IMAGES])
        tile_sel_sb = sb("tile_sel_sb", [IMAGES, NG * TILES])
        slot_sel_sb = sb("slot_sel_sb", [IMAGES, TT])
        steps_sb = sb("steps_sb", [IMAGES, ROUND + BLOCKS])

        h = sb("h", [TT, NG * TILES, DIM])
        stats = [sb(f"stats{i}", [TT, TILES, 6]) for i in range(2)]
        mean_var = [sb(f"mean_var{i}", [TT, TILES, 2]) for i in range(2)]
        var_eps = [sb(f"var_eps{i}", [TT, TILES]) for i in range(2)]
        rstd = [sb(f"rstd{i}", [TT, TILES]) for i in range(2)]
        neg_half = sb("neg_half", [TT, TILES])
        one = sb("one", [128, 1], F16)
        gelu_warm = sb("gelu_warm", [TT, TILES])
        eps_sb = sb("eps_sb", [TT, TILES])
        xn = [sb(f"xn{i}", [TT, TILES, DIM]) for i in range(2)]
        xn_t = sb("xn_t", [128, 3, GW], F16)
        q_room = sb("q_room", [128, 2 * GW])
        q_t = q_room[0:HD, :].rearrange("p (c t) -> p c t", c=2)
        k_t = sb("k_t", [HD, 2, GT])
        k_x = sb("k_x", [HD, 2, GI, HP, TOK])
        v_bd = sb("v_bd", [128, GI, HP, 2, HDIM])
        lora_in_sb = k_x[0:4, 0, 0:4, :, :].rearrange("p i a k -> p (i a k)")[:, 0:2 * 128 + 3 * DIM]
        lora_out_sb = k_x[0:4, 1, 0:4, :, :].rearrange("p i a k -> p (i a k)")[:, 0:2 * DIM]
        row_max = [sb(f"row_max{i}", [128, HEADS]) for i in range(2)]
        prob = [sb(f"prob{i}", [128, HEADS, SLOT]) for i in range(PAIRS)]
        row_sum = [sb(f"row_sum{i}", [128, HEADS]) for i in range(2)]
        inv_sum = [sb(f"inv_sum{i}", [128, HEADS]) for i in range(2)]
        prob_t = sb("prob_t", [128, HP, 2, TOK])
        att_t = sb("att_t", [HD, 2, GW])

        xs = sb("xs", [128, 3, IMAGES * TOK], F16)
        x_sum = sb("x_sum", [128, 2, IMAGES])
        sort_room = sb("sort_room", [128, (3 * BLOCKS * BW + 1) // 2])
        x_sorted = sort_room[:].bitcast(F16)[:, 0:3 * BLOCKS * BW].rearrange("p (q t) -> p q t", q=3)
        x1_sb = sort_room[:, 0:PK * GW].rearrange("p (k t) -> p k t", k=PK)
        logit = sb("logit", [IMAGES, EXPERTS])
        top = sb("top", [IMAGES, 1])
        logit_s = sb("logit_s", [IMAGES, EXPERTS])
        score_e = sb("score_e", [IMAGES, EXPERTS])
        score_s = sb("score_s", [IMAGES, 1])
        gate = sb("gate", [IMAGES, 1])
        is_top = sb("is_top", [IMAGES, EXPERTS])
        not_first = sb("not_first", [IMAGES, 1])
        chosen = sb("chosen", [IMAGES, EXPERTS])
        over = sb("over", [IMAGES, EXPERTS, ROUND])
        n_block = sb("n_block", [IMAGES, EXPERTS])
        start = sb("start", [IMAGES, EXPERTS])
        place_e = sb("place_e", [IMAGES, EXPERTS])
        place_c = sb("place_c", [IMAGES, EXPERTS])
        place = sb("place", [IMAGES, 1])
        gate_tile = sb("gate_tile", [IMAGES, NG * TILES])
        gate_tok = sb("gate_tok", [TT, NG * TILES])
        begun = sb("begun", [1, 2, BLOCKS])
        place_i = sb("place_i", [1, IMAGES], I32)
        expert_i = sb("expert_i", [1, BLOCKS], I32)
        hid = [sb(f"hid{i}", [128, BW]) for i in range(2)]
        hid_hl = early[:, 0:2 * FM * BW].bitcast(F16)\
            .rearrange("p (b k m t) -> p b k m t", b=2, k=2, m=FM)
        y_sorted = staged[:, 0:2 * BLOCKS * BW].rearrange("p (c t) -> p c t", c=2)
        y_rooms = (q_room[:], prob[0][:].rearrange("p a k -> p (a k)"))
        y_tile = [room[:, i * 2 * TT:(i + 1) * 2 * TT].rearrange("p (c t) -> p c t", c=2)
                  for room in y_rooms for i in range(3)]
        DEPTH = len(y_tile)
        out_sb = [xn[i][:, t, :] for i in range(2) for t in range(TILES)]
        OUTS = len(out_sb)

        x_loaded = sem("x_loaded")
        x1_loaded = sem("x1_loaded")
        embed_loaded = sem("embed_loaded")
        attn_loaded = sem("attn_loaded")
        lora_loaded = sem("lora_loaded")
        expert_loaded = sem("expert_loaded")
        zeroed = sem("zeroed")
        pos_added = sem("pos_added")
        mask_ready = sem("mask_ready")
        lora_done = sem("lora_done")
        qkv_full = sem("qkv_full")
        qkv_high = sem("qkv_high")
        qkv_low = sem("qkv_low")
        out_full = sem("out_full")
        embedded = sem("embedded")
        h_ready = sem("h_ready")
        stats_done = [sem(f"stats_done{i}") for i in range(2)]
        aggr_done = [sem(f"aggr_done{i}") for i in range(2)]
        eps_added = [sem(f"eps_added{i}") for i in range(2)]
        rstd_done = [sem(f"rstd_done{i}") for i in range(2)]
        xn_ready = [sem(f"xn_ready{i}") for i in range(2)]
        xn_turned = [sem(f"xn_turned{i}") for i in range(2)]
        xt_high = [sem(f"xt_high{i}") for i in range(2)]
        xt_low = [sem(f"xt_low{i}") for i in range(2)]
        token_sum = sem("token_sum")
        bias_added = sem("bias_added")
        q_done = sem("q_done")
        q_copied = sem("q_copied")
        k_done = sem("k_done")
        k_copied = sem("k_copied")
        k_spread_dve = sem("k_spread_dve")
        k_spread_pool = sem("k_spread_pool")
        v_done = sem("v_done")
        v_act = sem("v_act")
        v_dve = sem("v_dve")
        scored = sem("scored")
        max_done = sem("max_done")
        shift_done = sem("shift_done")
        exp_done = sem("exp_done")
        sum_done = sem("sum_done")
        inv_done = sem("inv_done")
        prob_ready = sem("prob_ready")
        prob_turned = sem("prob_turned")
        prob_copied = sem("prob_copied")
        att_done = sem("att_done")
        att_copied = sem("att_copied")
        projected = sem("projected")
        h2_ready = sem("h2_ready")
        w_scaled = sem("w_scaled")
        w_high = sem("w_high")
        w_low = sem("w_low")
        logits_done = sem("logits_done")
        routing = sem("routing")
        scores_exp = sem("scores_exp")
        ranked = sem("ranked")
        placed = sem("placed")
        gates_spread = sem("gates_spread")
        gates_ready = sem("gates_ready")
        places_ready = sem("places_ready")
        sorted_dve = sem("sorted_dve")
        sorted_act = sem("sorted_act")
        sorted_pool = sem("sorted_pool")
        hid_done = sem("hid_done")
        gelu_done = sem("gelu_done")
        hid_high = sem("hid_high")
        hid_low = sem("hid_low")
        y_done = sem("y_done")
        y_copied = sem("y_copied")
        picked_act = sem("picked_act")
        picked_dve = sem("picked_dve")
        y_turned = sem("y_turned")
        out_ready = sem("out_ready")
        stored = [sem(f"stored{i}") for i in range(2 * TILES)]

        block = ctx.enter_context(nc.Block())
        ATTN_LOADS = 5
        ACT_SORTS, DVE_SORTS, POOL_SORTS = (0, 3), (3, 6), (6, IMAGES // 8)
        V_BANK = (1, 2, 0, 1)
        POOL_HEADS = 3
        EXPERT_LOADS = 10
        W2A = EXPERTS * FM * 128
        w2b_pair = w2b_hl[:].rearrange("p (d k) -> p d k", k=2)
        SPLITS = ((w1_sb, w1_hl[:, 0, :], w1_hl[:, 1, :], EXPERTS * 2 * FFN // NG),
                  (w2_sb[:, 0:W2A], w2a_hl[:, 0, :], w2a_hl[:, 1, :], W2A // NG),
                  (w2_sb[:, W2A:], w2b_pair[:, :, 0], w2b_pair[:, :, 1], EXPERTS * FM * REST // NG))
        FEATURES = ((0, slice(0, 128)), (DIM - 128, slice(256 - DIM, 128)))
        LOW_ROWS = (slice(0, 128), slice(0, DIM - 128))
        TAILS = [GI - TI * t if GI < TI * (t + 1) else TI for t in range(TILES)]

        def spread(eng, c, a, b):
            n = b - a
            return eng.tensor_tensor(k_x[:, c, :, a:b, :],
                                     k_t[:, c, :].rearrange("p (i k) -> p i k", k=TOK).unsqueeze(2)
                                     .broadcast_to([HD, GI, n, TOK]),
                                     head_sel_sb[:, a:b].unsqueeze(1).unsqueeze(3).broadcast_to([HD, GI, n, TOK]),
                                     ALU.mult)

        def places(eng, regs, first):
            eng.load(regs, place_i[0:1, at(first, len(regs))])
            return [eng.snap(reg, min_val=0, max_val=(BLOCKS * BI - 1) * TOK) for reg in regs]

        def experts(eng, regs, j):
            eng.load(regs, expert_i[0:1, at(j, len(regs))])
            return [eng.snap(reg, min_val=0, max_val=EXPERTS - 1) for reg in regs]

        def is_first(g):
            return isinstance(g, int) and g == 0

        def is_late(g):
            return isinstance(g, int) and g >= NG - 2

        def is_last(g):
            return isinstance(g, int) and g == NG - 1

        @block.sync
        def _(sp):
            sp.dma_start(tok_w_sb[:], tok_w).then_inc(embed_loaded, 16)
            sp.dma_start(x_sb[:, :, 0:GT], x[0]).then_inc(x_loaded, 16)
            for dst, src in ((lora_in_sb, lora_in), (w_in_sb, w_in), (w_out_sb, w_out), (lora_out_sb, lora_out)):
                sp.dma_start(dst[:], src).then_inc(lora_loaded, 16)
            sp.dma_start(x1_sb[:, :, 0:GT], x[1]).then_inc(x1_loaded, 16)
            sp.dma_start(w1_sb[:], w1).then_inc(expert_loaded, 16)
            sp.wait_ge(embedded, 2)
            sp.dma_start(x_sb[:, :, 0:GT], x[2]).then_inc(x_loaded, 16)
            for dst, src in ((w2_sb, w2), (b1_sb, b1), (b2_sb, b2), (tile_sel_sb, tile_sel),
                             (slot_sel_sb, slot_sel), (steps_sb, steps), (fold_sb, fold), (wg_sb, wg), (order_sb, order)):
                sp.dma_start(dst[:], src).then_inc(expert_loaded, 16)
            with sp.Fori(3, NG) as g:
                sp.wait_ge(embedded, g * 2)
                sp.dma_start(x_sb[:, :, 0:GT], x[at(g, 1)].rearrange("a p k t -> (a p) k t")).then_inc(x_loaded, 16)
            for t in range(NG * TILES):
                n = TAILS[t % TILES] * TOK
                row = (t // TILES * GI + t % TILES * TI) * TOK
                sp.wait_ge(out_ready, t + 1)
                sp.dma_start(out[row:row + n, :], out_sb[t % OUTS][0:n, :]).then_inc(stored[t % OUTS], 16)
            for i in range(OUTS):
                sp.wait_ge(stored[i], 16 * (NG * TILES // OUTS))

        @block.gpsimd
        def _(pool):
            pool.memset(x_sb[:, :, GT:GW], 0.0).then_inc(zeroed, 1)
            pool.memset(x1_sb[:, :, GT:GW], 0.0).then_inc(zeroed, 1)
            pool.memset(neg_half[:], -0.5).then_inc(zeroed, 1)
            pool.memset(one[:], 1.0).then_inc(zeroed, 1)
            pool.memset(eps_sb[:], EPS).then_inc(zeroed, 1)
            pool.memset(v_bd[:], 0.0).then_inc(zeroed, 1)
            for i in range(PAIRS):
                pool.memset(prob[i][:], 0.0).then_inc(zeroed, 1)
            pool.memset(att_t[:, :, GT:GW], 0.0).then_inc(zeroed, 1)
            pool.wait_ge(embed_loaded, 16 * 3)
            pool.tensor_tensor(pos_sb[:], pos_sb[:], row_add_sb[:], ALU.add).then_inc(pos_added, 1)
            pool.wait_ge(attn_loaded, 16 * ATTN_LOADS)
            pool.tensor_copy(causal_sb[:], prob_t[:].rearrange("p a i k -> p (a i k)")).then_inc(mask_ready, 1)
            pool.tensor_copy(ident16_sb[:], ident32_sb[:]).then_inc(mask_ready, 1)

            def inverse_std(n, w):
                pool.wait_ge(aggr_done[w], TILES * n + TILES)
                pool.tensor_tensor(var_eps[w][:], mean_var[w][:, :, 1], eps_sb[:], ALU.add).then_inc(eps_added[w], 1)
                pool.wait_ge(eps_added[w], n + 1)
                pool.tensor_tensor(rstd[w][:], var_eps[w][:], neg_half[:], ALU.pow).then_inc(rstd_done[w], 1)

            def normalise(g, p):
                pool.wait_ge(inv_done, PAIRS * g + p + 1)
                pr = prob[p][:, :, 0:TOK]
                pool.tensor_tensor(pr, pr, inv_sum[p % 2][:].unsqueeze(2).broadcast_to([128, HEADS, TOK]),
                                   ALU.mult).then_inc(prob_ready, 1)

            def split_low(g):
                pool.wait_ge(w_high, g * 3 + 3)
                for w, high, low, n in SPLITS:
                    pool.tensor_tensor(low[:, at(g * n, n)], w[:, at(g * n, n)], high[:, at(g * n, n)],
                                       ALU.subtract).then_inc(w_low, 1)

            def add_out_bias(n):
                pool.wait_ge(xn_ready[0], TILES * n + TILES)
                ht = h[:, at(n * TILES, TILES), :]
                pool.tensor_tensor(ht, ht, b_out_sb[:].unsqueeze(1).broadcast_to([TT, TILES, DIM]), ALU.add)\
                    .then_inc(bias_added, 1)

            def spread_keys(n):
                for c in range(2):
                    pool.wait_ge(k_copied, n * 2 + c + 1)
                    spread(pool, c, POOL_HEADS, HP).then_inc(k_spread_pool, 1)

            def group(g):
                normalise(g, 0)
                normalise(g, 1)
                if not is_first(g):
                    inverse_std(g - 1, 1)
                normalise(g, 2)
                if not is_late(g):
                    inverse_std(g + 2, 0)
                if not is_last(g):
                    spread_keys(g + 1)
                normalise(g, 3)
                if not is_late(g):
                    add_out_bias(g + 2)
                split_low(g)

            inverse_std(0, 0)
            add_out_bias(0)
            inverse_std(1, 0)
            spread_keys(0)
            add_out_bias(1)
            pool.wait_ge(embedded, 4)
            pool.memset(sort_room[:, 0:PK * GW], 0.0).then_inc(zeroed, 1)
            pool.wait_ge(zeroed, 13)
            group(0)
            group(1)
            with pool.Fori(2, NG - 2) as g:
                group(g)
            group(NG - 2)
            group(NG - 1)
            inverse_std(NG - 1, 1)

            pool.wait_ge(places_ready, 2)
            pool.wait_ge(zeroed, 13)
            pool.wait_ge(xt_high[1], 2 * NG)
            pool.wait_ge(xt_low[1], 2 * NG)
            place_regs = [pool.alloc_register(f"pool_place{i}") for i in range(8)]
            with pool.Fori(*POOL_SORTS) as b:
                for k, to in enumerate(places(pool, place_regs, b * 8)):
                    pool.tensor_tensor(x_sorted[:, :, at(to, TOK)], xs[:, :, at((b * 8 + k) * TOK, TOK)],
                                       one[:].unsqueeze(2).broadcast_to([128, 3, TOK]), ALU.mult)\
                        .then_inc(sorted_pool, 1)

        @block.scalar
        def _(act):
            for dst, src in ((row_add_sb, row_add), (pos_sb, pos_rows)):
                act.dma_start(dst[:], src).then_inc(embed_loaded, 16)
            for dst, src in ((ident32_sb, ident32), (b_qkv_sb, b_qkv), (b_out_sb, b_out), (head_sel_sb, head_sel),
                             (prob_t.rearrange("p a i k -> p (a i k)"), causal)):
                act.dma_start(dst[:], src).then_inc(attn_loaded, 16)

            def copy_halves(n):
                for c, (_, rows) in enumerate(FEATURES):
                    act.wait_ge(xn_turned[0], 2 * n + c + 1)
                    act.activation(xn_t[rows, 2 * c, :], work_ps[1 + c][rows, 0:GW], ACT.Copy)\
                        .then_inc(xt_high[0], 1)

            def copy_q(n):
                for c in range(2):
                    act.wait_ge(q_done, 2 * n + c + 1)
                    act.activation(q_t[:, c, :], work_ps[1 + c][0:HD, 0:GW], ACT.Identity, bias=b_qkv_sb[:, c:c + 1],
                                   scale=1.0 / SPLIT).then_inc(q_copied, 1)

            def copy_k(n):
                for c in range(2):
                    act.wait_ge(k_done, 2 * n + c + 1)
                    act.activation(k_t[:, c, :], work_ps[c][0:HD, 0:GT], ACT.Identity, bias=b_qkv_sb[:, 2 + c:3 + c],
                                   scale=1.0 / SPLIT).then_inc(k_copied, 1)

            def copy_v(n, pairs):
                for j in pairs:
                    act.wait_ge(v_done, PAIRS * n + j + 1)
                    if not is_first(n):
                        act.wait_ge(att_done, PAIRS * (n - 1) + j + 1)
                    src = work_ps[V_BANK[j]][0:TOK, 0:DIM].rearrange("p (a b d) -> p a b d", b=2, d=HDIM)
                    for b in range(2):
                        act.activation(v_bd[SLOT * b:SLOT * b + TOK, 2 * j, :, b, :], src[:, :, b, :], ACT.Copy,
                                       scale=1.0 / SPLIT).then_inc(v_act, 1)

            def exps(g, p):
                act.wait_ge(shift_done, PAIRS * g + p + 1)
                act.activation(prob[p][:, :, 0:TOK], prob[p][:, :, 0:TOK], ACT.Exp).then_inc(exp_done, 1)

            def copy_prob(g, p):
                for s in range(2):
                    act.wait_ge(prob_turned, 2 * (PAIRS * g + p) + s + 1)
                    src = turn_ps[s][:, 0:384].rearrange("p (a i t) -> p a i t", a=3, i=2)[:, :, :, 0:TOK]
                    act.activation(prob_t[:, 3 * s:3 * s + 3, :, :], src, ACT.Copy).then_inc(prob_copied, 1)

            def copy_att(g):
                act.wait_ge(att_done, PAIRS * g + PAIRS)
                for c in range(2):
                    act.activation(att_t[:, c, 0:GT], att_ps[c][0:HD, 0:GT], ACT.Identity,
                                   bias=b_qkv_sb[:, 4 + c:5 + c]).then_inc(att_copied, 1)

            def copy_att_last(part):
                a, b = ((0, 2 * TT), (2 * TT, GT))[part]
                act.wait_ge(att_done, PAIRS * (NG - 1) + 3 + part)
                for c in range(2):
                    act.activation(att_t[:, c, a:b], att_ps[c][0:HD, a:b], ACT.Identity,
                                   bias=b_qkv_sb[:, 4 + c:5 + c]).then_inc(att_copied, 1)

            def copy_high2(n):
                for c, (_, rows) in enumerate(FEATURES):
                    act.wait_ge(xn_turned[1], 2 * n + c + 1)
                    act.activation(xs[rows, 2 * c, at(n * GT, GT)], work_ps[2 - c][rows, 0:GT], ACT.Copy)\
                        .then_inc(xt_high[1], 1)

            def split_high(g):
                if is_first(g):
                    act.wait_ge(expert_loaded, 16 * EXPERT_LOADS)
                for w, _, _, n in SPLITS:
                    act.activation(w[:, at(g * n, n)], w[:, at(g * n, n)], ACT.Copy, scale=SPLIT).then_inc(w_scaled, 1)
                act.wait_ge(w_scaled, g * 3 + 3)
                for w, high, _, n in SPLITS:
                    act.activation(high[:, at(g * n, n)], w[:, at(g * n, n)], ACT.Copy).then_inc(w_high, 1)

            def group(g):
                if not is_first(g):
                    copy_prob(g - 1, 2)
                    copy_prob(g - 1, 3)
                exps(g, 0)
                copy_v(g, range(3))
                if not is_first(g):
                    copy_att(g - 1)
                copy_v(g, (3,))
                copy_prob(g, 0)
                exps(g, 1)
                if not is_last(g):
                    copy_halves(g + 1)
                copy_prob(g, 1)
                exps(g, 2)
                split_high(g)
                if not is_last(g):
                    copy_q(g + 1)
                if not is_last(g):
                    copy_k(g + 1)
                exps(g, 3)
                if not is_first(g):
                    copy_high2(g - 1)

            act.wait_ge(qkv_full, 4)
            act.activation(qkv_hl[:, 0, :, :], w_in_sb[:], ACT.Copy, scale=SPLIT).then_inc(qkv_high, 1)
            copy_halves(0)
            copy_q(0)
            copy_k(0)
            act.wait_ge(zeroed, 12)
            group(0)
            group(1)
            with act.Fori(2, NG - 2) as g:
                group(g)
            group(NG - 2)
            group(NG - 1)
            copy_prob(NG - 1, 2)
            copy_att_last(0)
            copy_prob(NG - 1, 3)
            copy_att_last(1)
            copy_high2(NG - 1)

            act.wait_ge(routing, 3)
            act.activation(score_e[:], logit_s[:], ACT.Exp).then_inc(scores_exp, 1)

            act.wait_ge(zeroed, 12)
            act.activation(gelu_warm[:], neg_half[:], ACT.Gelu)

            act.wait_ge(places_ready, 2)
            act.wait_ge(xt_low[1], 2 * NG)
            place_regs = [act.alloc_register(f"act_place{i}") for i in range(8)]
            with act.Fori(*ACT_SORTS) as b:
                for k, to in enumerate(places(act, place_regs, b * 8)):
                    act.activation(x_sorted[:, :, at(to, TOK)], xs[:, :, at((b * 8 + k) * TOK, TOK)], ACT.Copy)\
                        .then_inc(sorted_act, 1)

            def gelu(j, e, first):
                for m in range(FM):
                    act.wait_ge(hid_done, j * FM + m + 1)
                    if not (first and m < 2):
                        act.wait_ge(hid_low, j * FM + (m - 1))
                    act.activation(hid[m % 2][:], gelu_ps[m][:, 0:BW], ACT.Gelu, bias=b1_sb[:, at(e * FM + m, 1)],
                                   scale=1.0 / SPLIT).then_inc(gelu_done, 1)

            def copy_y(j, e):
                for c in range(2):
                    act.wait_ge(y_done, j * 2 + c + 1)
                    act.activation(y_sorted[:, c, at(j * BW, BW)], y_ps[c][:, 0:BW], ACT.Identity,
                                   bias=b2_sb[:, at(e * 2 + c, 1)], scale=1.0 / SPLIT).then_inc(y_copied, 1)

            expert_regs = [act.alloc_register(f"act_expert{i}") for i in range(2)]
            gelu(0, experts(act, expert_regs, 0)[0], True)
            with act.Fori(1, BLOCKS) as j:
                e0, e1 = experts(act, expert_regs, j - 1)
                gelu(j, e1, False)
                copy_y(j - 1, e0)
            copy_y(BLOCKS - 1, experts(act, expert_regs, BLOCKS - 2)[1])

            for c in range(2):
                act.wait_ge(y_copied, 2 * BLOCKS)
            for t in range(NG * TILES):
                if t % TILES == 0:
                    of = places(act, place_regs, t // TILES * GI)
                if t >= DEPTH:
                    act.wait_ge(y_turned, t - DEPTH + 1)
                for k in range(2):
                    act.activation(y_tile[t % DEPTH][:, :, k * TOK:(k + 1) * TOK],
                                   y_sorted[:, :, at(of[t % TILES * TI + k], TOK)], ACT.Copy).then_inc(picked_act, 1)

        @block.tensor
        def _(pe):
            def wait_for(*counts):
                for signal, count in counts:
                    pe.wait_ge(signal, count)

            def embed(n, part, *free):
                patches = x_sb
                if isinstance(n, int) and n == 1:
                    patches = x1_sb
                    pe.wait_ge(x1_loaded, 16)
                elif is_first(n):
                    pe.wait_ge(x_loaded, 16)
                else:
                    pe.wait_ge(x_loaded, n * 16)
                wait_for(*free)
                for i, t in enumerate(((0, 1), (2,))[part]):
                    for k in range(PK):
                        mm = pe.matmul(work_ps[0][0:TT, i * DIM:(i + 1) * DIM], patches[:, k, t * TT:(t + 1) * TT],
                                       tok_w_sb[:, k, :], start=(k == 0), stop=(k == PK - 1))
                mm.then_inc(embedded, 1)

            def turn(n, w, banks, *free):
                pe.wait_ge(xn_ready[w], n * TILES + TILES)
                for c, (f0, _) in enumerate(FEATURES):
                    wait_for(*free[c])
                    for t in range(TILES):
                        mm = pe.transpose(work_ps[banks[c]][:, t * TT:(t + 1) * TT],
                                          xn[w][:, t, f0:f0 + 128], ident32_sb[0:TT, 0:TT])
                    mm.then_inc(xn_turned[w], 1)

            def queries_keys(n, *free):
                pe.wait_ge(xt_low[0], n * 2 + 2)
                pe.wait_ge(xt_high[0], n * 2 + 2)
                for o, c, cols, bank, done in ((0, 0, GW, 1, q_done), (0, 1, GW, 2, q_done),
                                               (DIM, 0, GT, 0, k_done), (DIM, 1, GT, 1, k_done)):
                    if done is k_done and c == 0:
                        wait_for(*free)
                    if done is k_done and c == 1:
                        pe.wait_ge(q_copied, n * 2 + 1)
                    for i, (wh, kc, slot) in enumerate(PARTS):
                        mm = pe.matmul(work_ps[bank][0:HD, 0:cols],
                                       qkv_hl[:, wh, kc, o + c * HD:o + (c + 1) * HD],
                                       xn_t[:, slot, 0:cols], start=(i == 0), stop=(i == len(PARTS) - 1))
                    mm.then_inc(done, 1)

            def values(n, pairs, *free):
                for j in pairs:
                    wait_for(*(free[j] if j < 3 else pair_out(n, 0)))
                    for b in range(2):
                        t0 = (2 * j + b) * TOK
                        for i, (wh, kc, slot) in enumerate(PARTS):
                            mm = pe.matmul(work_ps[V_BANK[j]][SLOT * b:SLOT * b + SLOT, 0:DIM],
                                           xn_t[:, slot, t0:t0 + SLOT], qkv_hl[:, wh, kc, 2 * DIM:3 * DIM],
                                           start=(i == 0), stop=(i == len(PARTS) - 1))
                    mm.then_inc(v_done, 1)

            def scores(g, p):
                if p == 0:
                    for s in (k_spread_dve, k_spread_pool, q_copied):
                        pe.wait_ge(s, g * 2 + 2)
                if not (is_first(g) and p == 0):
                    pe.wait_ge(shift_done, g * PAIRS + p)
                s = score_ps
                pe.matmul(s[:, 0:HEADS * TOK], ident16_sb[:], causal_sb[:], start=True, stop=True)
                for i in range(2):
                    im = 2 * p + i
                    for c in range(2):
                        mm = pe.matmul(s[SLOT * i:SLOT * i + SLOT, c * HP * TOK:(c + 1) * HP * TOK],
                                       q_t[:, c, im * TOK:im * TOK + SLOT], k_x[:, c, im, :, :],
                                       start=False, stop=True, skip_group_check=True)
                mm.then_inc(scored, 1)

            def turn_prob(g, p):
                pe.wait_ge(prob_ready, g * PAIRS + p + 1)
                for s in range(2):
                    if not (is_first(g) and p == 0):
                        pe.wait_ge(prob_copied, (g * PAIRS + p - 1) * 2 + s + 1)
                    for a in range(3):
                        i = 3 * s + a
                        mm = pe.transpose(turn_ps[s][:, a * 128:(a + 1) * 128], prob[p][:, 2 * i:2 * i + 2, :],
                                          ident32_sb[:])
                    mm.then_inc(prob_turned, 1)

            def weigh(g, p):
                pe.wait_ge(prob_copied, (g * PAIRS + p) * 2 + 2)
                if p == 0:
                    pe.wait_ge(v_act, g * 2 * PAIRS + 2 * PAIRS)
                    pe.wait_ge(v_dve, g * 2 * PAIRS + 2 * PAIRS)
                    if not is_first(g):
                        pe.wait_ge(att_copied, g * 2)
                for i in range(2):
                    im = 2 * p + i
                    for a in range(HP):
                        r = 32 * (a % 3)
                        mm = pe.matmul(att_ps[a // 3][r:r + 32, im * TOK:(im + 1) * TOK],
                                       v_bd[:, im, a, :, :], prob_t[:, a, i, :], start=True, stop=True)
                mm.then_inc(att_done, 1)

            def project(n, *free, parts=(0, 1)):
                for part in parts:
                    bank, tiles = ((2, (0, 1)), (0, (2,)))[part]
                    pe.wait_ge(att_copied, n * 2 + (4 if parts == (1,) else 2))
                    wait_for(*free[part])
                    for i, t in enumerate(tiles):
                        for c in range(2):
                            mm = pe.matmul(work_ps[bank][0:TT, i * DIM:(i + 1) * DIM],
                                           att_t[:, c, t * TT:(t + 1) * TT], w_out_sb[:, c, :],
                                           start=(c == 0), stop=(c == 1))
                    mm.then_inc(projected, 1)

            def pair_out(n, j):
                return (v_act, n * 2 * PAIRS + 2 * j + 2), (v_dve, n * 2 * PAIRS + 2 * j + 2)

            def turned_out(n, w, c):
                sums = ((token_sum, n * 2 + c + 1),) if w else ()
                return (xt_high[w], n * 2 + c + 1), (xt_low[w], n * 2 + c + 1), *sums

            def group(g):
                if not is_first(g):
                    turn_prob(g - 1, 2)
                if not is_late(g):
                    embed(g + 2, 0, (k_copied, g * 2 + 1))
                if not is_first(g):
                    weigh(g - 1, 2)
                scores(g, 0)
                if not is_first(g):
                    turn_prob(g - 1, 3)
                third = (k_copied, g * 2 + 1) if is_late(g) else (h_ready, g * 2 + 5)
                if isinstance(g, int) and g < 2:
                    values(g, range(3), ((k_copied, g * 2 + 2),), ((q_copied, g * 2 + 2),), (third,))
                else:
                    values(g, range(3), turned_out(g - 2, 1, 1), turned_out(g - 2, 1, 0), (third,))
                if not is_first(g):
                    weigh(g - 1, 3)
                scores(g, 1)
                values(g, (3,))
                turn_prob(g, 0)
                if not is_first(g):
                    project(g - 1, pair_out(g, 1), pair_out(g, 2))
                weigh(g, 0)
                if not is_last(g):
                    turn(g + 1, 0, (1, 2), pair_out(g, 3),
                         pair_out(g, 1) if is_first(g) else ((h2_ready, g * 2 - 1),))
                scores(g, 2)
                turn_prob(g, 1)
                if not is_late(g):
                    embed(g + 2, 1, *(pair_out(g, 2) if is_first(g) else ((h2_ready, g * 2),)))
                weigh(g, 1)
                scores(g, 3)
                if not is_last(g):
                    queries_keys(g + 1, (h2_ready, g * 2) if is_late(g) else (h_ready, g * 2 + 6))
                if is_last(g):
                    turn(g - 1, 1, (2, 1), ((h2_ready, g * 2 - 1),), pair_out(g, 3))
                elif not is_first(g):
                    turn(g - 1, 1, (2, 1), ((q_copied, g * 2 + 4),), ((k_copied, g * 2 + 4),))

            pe.wait_ge(zeroed, 12)
            pe.wait_ge(embed_loaded, 16 * 3)
            embed(0, 0)
            pe.wait_ge(lora_loaded, 16 * 4)
            for kc in range(2):
                for s in range(2):
                    pe.matmul(lora_ps[2 * kc + s][:, 0:288], lora_in_sb[:, kc * 128:(kc + 1) * 128],
                              lora_in_sb[:, 256 + s * 288:256 + (s + 1) * 288], start=True, stop=True)\
                        .then_inc(lora_done, 1)
            for kc in range(2):
                pe.matmul(turn_ps[kc][0:HD, 0:DIM], lora_out_sb[:, kc * HD:(kc + 1) * HD],
                          lora_out_sb[:, DIM:2 * DIM], start=True, stop=True).then_inc(lora_done, 1)
            embed(0, 1, (h_ready, 1))
            embed(1, 0, (h_ready, 2))
            pe.wait_ge(attn_loaded, 16 * ATTN_LOADS)
            turn(0, 0, (1, 2), ((qkv_full, 4),), ((qkv_full, 4),))
            embed(1, 1, (h_ready, 3))
            pe.wait_ge(qkv_high, 1)
            pe.wait_ge(qkv_low, 1)
            queries_keys(0, (h_ready, 4))
            pe.wait_ge(out_full, 2)
            pe.wait_ge(mask_ready, 2)
            group(0)
            group(1)
            with pe.Fori(2, NG - 2) as g:
                group(g)
            group(NG - 2)
            group(NG - 1)
            turn_prob(NG - 1, 2)
            weigh(NG - 1, 2)
            turn_prob(NG - 1, 3)
            project_free = (turned_out(NG - 2, 1, 0), ((h2_ready, NG * 2 - 2),))
            project(NG - 1, *project_free, parts=(0,))
            weigh(NG - 1, 3)
            project(NG - 1, *project_free, parts=(1,))
            turn(NG - 1, 1, (2, 1), ((h2_ready, NG * 2 - 1),), turned_out(NG - 2, 1, 1))

            pe.wait_ge(token_sum, 2 * NG)
            pe.wait_ge(expert_loaded, 16 * EXPERT_LOADS)
            for c, (_, rows) in enumerate(FEATURES):
                mm = pe.matmul(score_ps[0:IMAGES, 0:EXPERTS], x_sum[rows, c, :], wg_sb[rows, c, :],
                               start=(c == 0), stop=(c == 1))
            mm.then_inc(logits_done, 1)
            pe.wait_ge(routing, 8)
            pe.wait_ge(expert_loaded, 16 * EXPERT_LOADS)
            pe.matmul(att_ps[0][0:IMAGES, 0:EXPERTS], order_sb[:, 0:IMAGES], chosen[:], start=True, stop=True)
            pe.matmul(att_ps[0][0:IMAGES, EXPERTS:2 * EXPERTS], order_sb[:, IMAGES:2 * IMAGES], chosen[:],
                      start=True, stop=True).then_inc(ranked, 1)
            pe.wait_ge(placed, 1)
            pe.matmul(turn_ps[0][0:1, 0:IMAGES], place[:], ident32_sb[0:IMAGES, 0:IMAGES], start=True, stop=True)\
                .then_inc(gates_spread, 1)
            pe.matmul(turn_ps[1][0:TT, 0:NG * TILES], slot_sel_sb[:], gate_tile[:], start=True, stop=True)\
                .then_inc(gates_spread, 1)

            expert_regs = [pe.alloc_register(f"pe_expert{i}") for i in range(3)]

            def hidden(j, e, m, first):
                if not first:
                    pe.wait_ge(gelu_done, j * FM + (m + 1 - FM))
                for i, (wh, kc, slot) in enumerate(PARTS):
                    mm = pe.matmul(gelu_ps[m][:, 0:BW],
                                   w1_hl[:, wh, at(e * (2 * FFN) + (kc * FFN + m * 128), 128)],
                                   x_sorted[:, slot, at(j * BW, BW)], start=(i == 0), stop=(i == len(PARTS) - 1))
                mm.then_inc(hid_done, 1)

            def outputs(j, e, par, m, first):
                pe.wait_ge(hid_low, j * FM + (m + 1))
                for c in range(2):
                    if m == 0 and not first:
                        pe.wait_ge(y_copied, j * 2 + c - 1)
                    terms = ((w2a_hl[:, 0, :], 0), (w2a_hl[:, 0, :], 1), (w2a_hl[:, 1, :], 0)) if c == 0 else \
                        ((w2b_hl, 0), (w2b_hl, 1))
                    for i, (w, xh) in enumerate(terms):
                        mm = pe.matmul(y_ps[c][:, 0:BW], w[:, at(e * (FM * 128) + m * 128, 128)],
                                       hid_hl[:, par, xh, m, :],
                                       start=(m == 0 and i == 0), stop=(m == FM - 1 and i == len(terms) - 1),
                                       skip_group_check=True)
                    if m == FM - 1:
                        mm.then_inc(y_done, 1)

            pe.wait_ge(places_ready, 2)
            pe.wait_ge(gates_ready, 1)
            for signal, (first, last) in ((sorted_dve, DVE_SORTS), (sorted_act, ACT_SORTS), (sorted_pool, POOL_SORTS)):
                pe.wait_ge(signal, 8 * (last - first))
            pe.wait_ge(w_low, 3 * NG)
            pe.wait_ge(w_high, 3 * NG)
            def beside(j, e0, e1, par, first=False):
                for m in range(FM):
                    hidden(j, e1, m, False)
                    outputs(j - 1, e0, par, m, first)

            e = experts(pe, expert_regs, 0)
            for m in range(FM):
                hidden(0, e[0], m, True)
            beside(1, e[0], e[1], 0, True)
            beside(2, e[1], e[2], 1)
            with pe.Fori(0, (BLOCKS - 3) // 2) as b:
                j = b * 2 + 3
                e = experts(pe, expert_regs, j - 1)
                beside(j, e[0], e[1], 0)
                beside(j + 1, e[1], e[2], 1)
            e = experts(pe, expert_regs, BLOCKS - 3)
            for m in range(FM):
                outputs(BLOCKS - 1, e[2], (BLOCKS - 1) % 2, m, False)

            for t in range(NG * TILES):
                pe.wait_ge(picked_act, 2 * t + 2)
                pe.wait_ge(picked_dve, t + 1)
                if t >= DEPTH:
                    pe.wait_ge(out_ready, t - DEPTH + 1)
                pe.transpose(gelu_ps[t % DEPTH][0:TT, 0:128], y_tile[t % DEPTH][:, 0, :], ident32_sb[:])
                mm = pe.matmul(gelu_ps[t % DEPTH][0:TT, 128:DIM], y_tile[t % DEPTH][:, 1, :], fold_sb[:],
                               start=True, stop=True)
                mm.then_inc(y_turned, 1)

        @block.vector
        def _(dve):
            def add_positions(n, part):
                a, b = ((0, 2), (2, 1))[part]
                dve.wait_ge(embedded, n * 2 + part + 1)
                dve.tensor_tensor(h[:, at(n * TILES + a, b), :],
                                  work_ps[0][0:TT, 0:b * DIM].rearrange("p (a d) -> p a d", d=DIM),
                                  pos_sb[:].unsqueeze(1).broadcast_to([TT, b, DIM]), ALU.add).then_inc(h_ready, 1)

            def add_attention(n):
                dve.wait_ge(bias_added, n + 1)
                for part, (a, b) in enumerate(((0, 2), (2, 1))):
                    dve.wait_ge(projected, n * 2 + part + 1)
                    dve.tensor_tensor(h[:, at(n * TILES + a, b), :],
                                      work_ps[2 - 2 * part][0:TT, 0:b * DIM].rearrange("p (a d) -> p a d", d=DIM),
                                      h[:, at(n * TILES + a, b), :], ALU.add).then_inc(h2_ready, 1)

            def moments(n, w):
                dve.wait_ge(attn_loaded, 16 * ATTN_LOADS)
                dve.wait_ge((h_ready, h2_ready)[w], n * 2 + 2)
                for t in range(TILES):
                    dve.bn_stats(stats[w][:, t, :], h[:, at(n * TILES + t, 1), :].rearrange("p a d -> p (a d)"))\
                        .then_inc(stats_done[w], 1)
                dve.wait_ge(stats_done[w], n * TILES + TILES)

            def aggregate(w):
                for t in range(TILES):
                    dve.bn_aggr(mean_var[w][:, t, :], stats[w][:, t, :]).then_inc(aggr_done[w], 1)

            def norm(n, w):
                dve.wait_ge(rstd_done[w], n + 1)
                if not is_first(n):
                    dve.wait_ge(xn_turned[w], n * 2)
                for t in range(TILES):
                    dve.tensor_scalar(xn[w][:, t, :], h[:, at(n * TILES + t, 1), :].rearrange("p a d -> p (a d)"),
                                      mean_var[w][:, t, 0:1], rstd[w][:, t:t + 1], ALU.subtract, ALU.mult)\
                        .then_inc(xn_ready[w], 1)

            def low_halves(n):
                for c, (_, rows) in enumerate(FEATURES):
                    dve.wait_ge(xt_high[0], n * 2 + c + 1)
                    low = xn_t[LOW_ROWS[c], 1 + c, :]
                    dve.tensor_tensor(low, work_ps[1 + c][rows, 0:GW], xn_t[rows, 2 * c, :], ALU.subtract)\
                        .then_inc(xt_low[0], 1)

            def low_halves2(n):
                for c, (_, rows) in enumerate(FEATURES):
                    dve.wait_ge(xt_high[1], n * 2 + c + 1)
                    dve.tensor_tensor(xs[LOW_ROWS[c], 1 + c, at(n * GT, GT)], work_ps[2 - c][rows, 0:GT],
                                      xs[rows, 2 * c, at(n * GT, GT)], ALU.subtract).then_inc(xt_low[1], 1)
                    dve.tensor_reduce(x_sum[rows, c, at(n * GI, GI)],
                                      work_ps[2 - c][rows, 0:GT].rearrange("p (i k) -> p i k", k=TOK), AX, ALU.add)\
                        .then_inc(token_sum, 1)

            def spread_keys(n):
                for c in range(2):
                    dve.wait_ge(k_copied, n * 2 + c + 1)
                    spread(dve, c, 0, POOL_HEADS).then_inc(k_spread_dve, 1)

            def copy_v(n, pairs):
                for j in pairs:
                    dve.wait_ge(v_act, n * 2 * PAIRS + 2 * j + 2)
                    if not is_first(n):
                        dve.wait_ge(att_done, PAIRS * (n - 1) + j + 1)
                    src = work_ps[V_BANK[j]][SLOT:SLOT + TOK, 0:DIM].rearrange("p (a b d) -> p a b d", b=2, d=HDIM)
                    for b in range(2):
                        dve.tensor_scalar(v_bd[SLOT * b:SLOT * b + TOK, 2 * j + 1, :, b, :], src[:, :, b, :],
                                          1.0 / SPLIT, None, ALU.mult).then_inc(v_dve, 1)

            def shift(g, p):
                s = score_ps[:, 0:HEADS * TOK].rearrange("p (a k) -> p a k", k=TOK)
                dve.wait_ge(scored, g * PAIRS + p + 1)
                dve.tensor_reduce(row_max[p % 2][:], s, AX, ALU.max).then_inc(max_done, 1)
                dve.wait_ge(max_done, g * PAIRS + p + 1)
                if not is_first(g):
                    dve.wait_ge(prob_turned, 2 * PAIRS * (g - 1) + 2 * p + 2)
                dve.tensor_tensor(prob[p][:, :, 0:TOK], s,
                                  row_max[p % 2][:].unsqueeze(2).broadcast_to([128, HEADS, TOK]), ALU.subtract)\
                    .then_inc(shift_done, 1)

            def sums(g, p):
                dve.wait_ge(exp_done, g * PAIRS + p + 1)
                dve.tensor_reduce(row_sum[p % 2][:], prob[p][:, :, 0:TOK], AX, ALU.add).then_inc(sum_done, 1)
                dve.wait_ge(sum_done, g * PAIRS + p + 1)
                if not (is_first(g) and p < 2):
                    dve.wait_ge(prob_ready, g * PAIRS + (p - 1))
                dve.reciprocal(inv_sum[p % 2][:], row_sum[p % 2][:]).then_inc(inv_done, 1)

            def group(g):
                if not is_late(g):
                    add_positions(g + 2, 0)
                shift(g, 0)
                sums(g, 0)
                copy_v(g, range(3))
                shift(g, 1)
                copy_v(g, (3,))
                sums(g, 1)
                if not is_first(g):
                    add_attention(g - 1)
                    moments(g - 1, 1)
                if not is_last(g):
                    low_halves(g + 1)
                if not is_first(g):
                    aggregate(1)
                shift(g, 2)
                if not is_late(g):
                    add_positions(g + 2, 1)
                    moments(g + 2, 0)
                sums(g, 2)
                if not is_first(g):
                    norm(g - 1, 1)
                if not is_late(g):
                    aggregate(0)
                shift(g, 3)
                if not is_late(g):
                    norm(g + 2, 0)
                if not is_last(g):
                    spread_keys(g + 1)
                sums(g, 3)
                if not is_first(g):
                    low_halves2(g - 1)

            dve.memset(sort_room[:, PK * GW:], 0.0).then_inc(zeroed, 1)
            dve.wait_ge(pos_added, 1)
            add_positions(0, 0)
            dve.wait_ge(lora_loaded, 16 * 4)
            for kc in range(2):
                for s in range(2):
                    dve.wait_ge(lora_done, 2 * kc + s + 1)
                    w = w_in_sb[:, kc, s * 288:(s + 1) * 288]
                    dve.scalar_tensor_tensor(out=w, in0=lora_ps[2 * kc + s][:, 0:288], scalar=LORA, in1=w,
                                             op0=ALU.mult, op1=ALU.add).then_inc(qkv_full, 1)
            add_positions(0, 1)
            moments(0, 0)
            aggregate(0)
            dve.wait_ge(qkv_high, 1)
            dve.scalar_tensor_tensor(out=qkv_hl[:, 1, :, :], in0=w_in_sb[:], scalar=SPLIT, in1=qkv_hl[:, 0, :, :],
                                     op0=ALU.mult, op1=ALU.subtract).then_inc(qkv_low, 1)
            norm(0, 0)
            add_positions(1, 0)
            low_halves(0)
            add_positions(1, 1)
            moments(1, 0)
            aggregate(0)
            dve.wait_ge(lora_done, 6)
            for kc in range(2):
                w = w_out_sb[:, kc, :]
                dve.scalar_tensor_tensor(out=w, in0=turn_ps[kc][0:HD, 0:DIM], scalar=LORA, in1=w,
                                         op0=ALU.mult, op1=ALU.add).then_inc(out_full, 1)
            spread_keys(0)
            norm(1, 0)
            dve.wait_ge(zeroed, 12)
            group(0)
            group(1)
            with dve.Fori(2, NG - 2) as g:
                group(g)
            group(NG - 2)
            group(NG - 1)
            add_attention(NG - 1)
            moments(NG - 1, 1)
            aggregate(1)
            norm(NG - 1, 1)
            low_halves2(NG - 1)

            step = 0

            def then(ins):
                nonlocal step
                step += 1
                ins.then_inc(routing, 1)
                dve.wait_ge(routing, step)

            dve.wait_ge(logits_done, 1)
            then(dve.tensor_scalar(logit[:], score_ps[0:IMAGES, 0:EXPERTS], 1.0 / TOK, None, ALU.mult))
            then(dve.tensor_reduce(top[:], logit[:], AX, ALU.max))
            then(dve.tensor_scalar(logit_s[:], logit[:], top[:], None, ALU.subtract))
            then(dve.tensor_scalar(is_top[:], logit[:], top[:], None, ALU.is_equal))
            then(dve.tensor_scalar(not_first[:], is_top[:, 0:1], -1.0, 1.0, ALU.mult, ALU.add))
            then(dve.tensor_copy(chosen[:, 0:1], is_top[:, 0:1]))
            then(dve.tensor_tensor(chosen[:, 1:2], is_top[:, 1:2], not_first[:], ALU.mult))
            then(dve.tensor_tensor(chosen[:, 2:3], not_first[:], chosen[:, 1:2], ALU.subtract))
            dve.wait_ge(scores_exp, 1)
            then(dve.tensor_reduce(score_s[:], score_e[:], AX, ALU.add))
            then(dve.reciprocal(gate[:], score_s[:]))
            dve.wait_ge(expert_loaded, 16 * EXPERT_LOADS)
            then(dve.tensor_scalar(gate_tile[:], tile_sel_sb[:], gate[:], None, ALU.mult))
            dve.wait_ge(ranked, 1)
            then(dve.tensor_tensor(over[:],
                                   att_ps[0][0:IMAGES, EXPERTS:2 * EXPERTS].unsqueeze(2)
                                   .broadcast_to([IMAGES, EXPERTS, ROUND]),
                                   steps_sb[:, 0:ROUND].unsqueeze(1).broadcast_to([IMAGES, EXPERTS, ROUND]),
                                   ALU.is_gt))
            then(dve.tensor_reduce(n_block[:], over[:], AX, ALU.add))
            then(dve.memset(start[:, 0:1], 0.0))
            then(dve.tensor_copy(start[:, 1:2], n_block[:, 0:1]))
            then(dve.tensor_tensor(start[:, 2:3], n_block[:, 0:1], n_block[:, 1:2], ALU.add))
            then(dve.scalar_tensor_tensor(out=place_e[:], in0=start[:], scalar=float(BI),
                                          in1=att_ps[0][0:IMAGES, 0:EXPERTS], op0=ALU.mult, op1=ALU.add))
            then(dve.scalar_tensor_tensor(out=place_c[:], in0=place_e[:], scalar=float(TOK), in1=chosen[:],
                                          op0=ALU.mult, op1=ALU.mult))
            dve.tensor_reduce(place[:], place_c[:], AX, ALU.add).then_inc(placed, 1)
            for k in range(2):
                then(dve.tensor_scalar(begun[:, k, :], steps_sb[0:1, ROUND:], start[0:1, k + 1:k + 2], None,
                                       ALU.is_ge))
            dve.tensor_tensor(expert_i[:], begun[:, 0, :], begun[:, 1, :], ALU.add).then_inc(places_ready, 1)
            dve.wait_ge(gates_spread, 1)
            dve.tensor_copy(place_i[:], turn_ps[0][0:1, 0:IMAGES]).then_inc(places_ready, 1)
            dve.wait_ge(gates_spread, 2)
            dve.tensor_copy(gate_tok[:], turn_ps[1][0:TT, 0:NG * TILES]).then_inc(gates_ready, 1)

            dve.wait_ge(places_ready, 2)
            dve.wait_ge(zeroed, 13)
            dve.wait_ge(xt_high[1], 2 * NG)
            dve.wait_ge(xt_low[1], 2 * NG)
            place_regs = [dve.alloc_register(f"dve_place{i}") for i in range(8)]
            with dve.Fori(*DVE_SORTS) as b:
                for k, to in enumerate(places(dve, place_regs, b * 8)):
                    dve.tensor_copy(x_sorted[:, :, at(to, TOK)], xs[:, :, at((b * 8 + k) * TOK, TOK)])\
                        .then_inc(sorted_dve, 1)

            def halves(j, par, first):
                if not first:
                    dve.wait_ge(y_done, j * 2 - 2)
                for m in range(FM):
                    hh, hl = (hid_hl[:, par, k, m, :] if isinstance(par, int) else
                              hid_hl[:, at(par, 1), k, m, :].rearrange("p a t -> p (a t)") for k in range(2))
                    dve.wait_ge(gelu_done, j * FM + (m + 1))
                    dve.tensor_copy(hh, hid[m % 2][:]).then_inc(hid_high, 1)
                    dve.wait_ge(hid_high, j * FM + (m + 1))
                    dve.tensor_tensor(hl, hid[m % 2][:], hh, ALU.subtract).then_inc(hid_low, 1)

            halves(0, 0, True)
            halves(1, 1, True)
            with dve.Fori(2, BLOCKS) as j:
                par = dve.snap(j & 1)
                halves(j, par, False)

            def pick(t, of):
                if t >= DEPTH:
                    dve.wait_ge(y_turned, t - DEPTH + 1)
                k = TI - 1
                at_k = of[min(t % TILES * TI + k, GI - 1)]
                dve.tensor_copy(y_tile[t % DEPTH][:, :, k * TOK:(k + 1) * TOK], y_sorted[:, :, at(at_k, TOK)])\
                    .then_inc(picked_dve, 1)

            dve.wait_ge(y_copied, 2 * BLOCKS)
            AHEAD = 3
            for t in range(NG * TILES + AHEAD):
                if t < NG * TILES:
                    if t % TILES == 0:
                        of = places(dve, place_regs, t // TILES * GI)
                    pick(t, of)
                u = t - AHEAD
                if u >= 0:
                    dve.wait_ge(y_turned, u + 1)
                    if u >= OUTS:
                        dve.wait_ge(stored[u % OUTS], 16 * (u // OUTS))
                    dve.scalar_tensor_tensor(out=out_sb[u % OUTS], in0=gelu_ps[u % DEPTH][0:TT, 0:DIM],
                                             scalar=gate_tok[:, u:u + 1], in1=h[:, u, :],
                                             op0=ALU.mult, op1=ALU.add).then_inc(out_ready, 1)


def _laid_out(x, L0_tok_W, L0_tok_b, L0_tok_cls_token, L0_tok_pos_table, L0_attn_w_in, L0_attn_b_in, L0_attn_A_in,
              L0_attn_B_in, L0_attn_w_out, L0_attn_b_out, L0_attn_A_out, L0_attn_B_out, L0_ffn_Wg, L0_ffn_W1,
              L0_ffn_b1, L0_ffn_W2, L0_ffn_b2):
    a = {k: np.asarray(v) for k, v in locals().items()}
    f = np.float32
    p = a["x"].reshape(IMAGES, GRID, PATCH, GRID, PATCH, 3).transpose(0, 1, 3, 2, 4, 5)
    p = p.reshape(IMAGES, TOK - 1, PIX)
    p = np.concatenate([np.zeros((IMAGES, 1, PIX), f), p], axis=1)
    cls = a["L0_tok_cls_token"].reshape(1, DIM)
    rows = np.concatenate([cls, np.broadcast_to(a["L0_tok_b"], (TOK - 1, DIM))], axis=0)
    b_in = a["L0_attn_b_in"].reshape(6, HD)
    image = np.arange(IMAGES)
    part = np.arange(HD)
    head_sel = (part[:, None] // HDIM == np.arange(HP)[None, :]).astype(f)
    q = np.arange(128)[:, None]
    k = np.tile(np.arange(TOK), HEADS)[None, :]
    hidden = (q % SLOT < TOK) & (k > q % SLOT)
    tile = image // GI * TILES + image % GI // TI
    slot = image % GI % TI
    w2 = a["L0_ffn_W2"].reshape(EXPERTS, FM, 128, DIM).transpose(2, 0, 1, 3)
    b2 = np.zeros((128, EXPERTS, 2), f)
    b2[:, :, 0] = a["L0_ffn_b2"][:, :128].T
    b2[::2, :, 1] = a["L0_ffn_b2"][:, 128:].T
    steps = np.concatenate([BI * np.arange(ROUND), np.arange(BLOCKS)]).astype(f)
    return {
        "x": p.reshape(NG, GT, PK, 128).transpose(0, 3, 2, 1),
        "tok_w": a["L0_tok_W"].reshape(PK, 128, DIM).transpose(1, 0, 2),
        "row_add": np.tile(rows, (TI, 1)),
        "pos_rows": np.tile(a["L0_tok_pos_table"], (TI, 1)),
        "w_in": _feature_chunks(a["L0_attn_w_in"]),
        "lora_in": np.concatenate([_feature_chunks(a["L0_attn_B_in"]).transpose(2, 1, 0).reshape(4, 256),
                                   a["L0_attn_A_in"]], axis=1),
        "w_out": a["L0_attn_w_out"].reshape(2, HD, DIM).transpose(1, 0, 2),
        "lora_out": np.concatenate([a["L0_attn_B_out"].T, a["L0_attn_A_out"]], axis=1),
        "b_qkv": b_in.T,
        "b_out": np.tile(a["L0_attn_b_out"][None, :], (TT, 1)),
        "head_sel": head_sel,
        "causal": np.where(hidden, -1e9, 0.0).astype(f),
        "ident32": np.eye(128, dtype=f),
        "wg": _feature_chunks(a["L0_ffn_Wg"].T),
        "w1": _feature_chunks(a["L0_ffn_W1"]).transpose(1, 0, 2, 3).reshape(128, -1),
        "b1": a["L0_ffn_b1"].reshape(EXPERTS * FM, 128).T,
        "w2": np.concatenate([w2[..., :128].reshape(128, -1), w2[..., 128:].reshape(128, -1)], axis=1),
        "b2": b2.reshape(128, EXPERTS * 2),
        "fold": (np.arange(128)[:, None] // 2 == np.arange(REST)[None, :]).astype(f),
        "order": np.concatenate([np.triu(np.ones((IMAGES, IMAGES)), 1), np.ones((IMAGES, IMAGES))], 1).astype(f),
        "tile_sel": (tile[:, None] == np.arange(NG * TILES)[None, :]).astype(f),
        "slot_sel": (slot[:, None] == np.arange(TT)[None, :] // TOK).astype(f),
        "steps": np.tile(steps[None, :], (IMAGES, 1)),
    }


def _feature_chunks(w):
    return np.stack([w[..., :128, :], np.concatenate([w[..., 128:, :]] * 2, axis=-2)], axis=-2)


def kernel(**inputs):
    import concourse.bacc as bacc
    from concourse.bass_utils import run_bass_kernel_spmd

    arrays = {k: np.ascontiguousarray(v) for k, v in _laid_out(**inputs).items()}
    nc = bacc.Bacc("TRN2", target_bir_lowering=False, num_devices=1)
    aps = {k: nc.dram_tensor(f"in_{k}", v.shape, mybir.dt.from_np(v.dtype), kind="ExternalInput").ap()
           for k, v in arrays.items()}
    out = nc.dram_tensor("out", (IMAGES * TOK, DIM), F32, kind="ExternalOutput").ap()
    vit_layer(nc, **aps, out=out)
    r = run_bass_kernel_spmd(nc, [{f"in_{k}": v for k, v in arrays.items()}], core_ids=[0])
    return r.results[0]["out"].reshape(IMAGES, TOK, DIM)
```
